# Optimizing a Trainium2 kernel written in Bass

```python
import numpy as np
import jax
import jax.numpy as jnp

def _softmax(x, axis=-1):
    return jax.nn.softmax(x, axis=axis)

def _gelu(x):
    return jax.nn.gelu(x, approximate=True)

def _silu(x):
    return jax.nn.silu(x)

def _sigmoid(x):
    return jax.nn.sigmoid(x)

def _layernorm(x, axis=-1, eps=1e-05):
    m = jnp.mean(x, axis=axis, keepdims=True)
    v = jnp.var(x, axis=axis, keepdims=True)
    return (x - m) / jnp.sqrt(v + eps)

def _scatter_add(tgt, idx, src, axis=0):
    return tgt.at[idx].add(src)

def _segment_sum(src, seg, n):
    return jax.ops.segment_sum(src, seg, n)
kernel_name = 'mk_adj_resnorm_d4_adj_r2_afd0e4'

def setup_inputs(seed: int=0):
    np.random.seed(seed)
    _w = jnp.asarray

    def _rec_inputs():
        import jax
        import jax.numpy as jnp
        _gk = jax.random.key(seed)
        x = -0.0002928 + 1 * jax.random.normal(jax.random.fold_in(_gk, 1), (16, 512, 128), jnp.float32)
        _a = jax.random.bernoulli(jax.random.fold_in(_gk, 2), 0.03125, (16, 512, 512))
        _a = jnp.logical_or(_a, jnp.swapaxes(_a, -1, -2))
        _a = jnp.logical_or(_a, jnp.eye(512, dtype=bool))
        _af = _a.astype(jnp.float32)
        _af = _af * jax.random.uniform(jax.random.fold_in(_gk, 3), (16, 512, 512), jnp.float32, 0.05, 1)
        adj = _af
        return (x, adj)
    x, adj = _rec_inputs()

    def _L0_gnn_setup():
        import jax, jax.numpy as jnp
        import numpy as np
        B, N, D, H = (8, 1024, 128, 512)
        RMS_EPS = 1e-06

        def _rmsnorm(h, w, eps=RMS_EPS):
            var = jnp.mean(jnp.square(h), axis=-1, keepdims=True)
            return h * jax.lax.rsqrt(var + eps) * w
        key = jax.random.key(seed)
        ks = jax.random.split(key, 5)
        x = jax.random.normal(ks[0], (B, N, D), dtype=jnp.float32)
        adjacency = jax.random.uniform(ks[1], (B, N, N), dtype=jnp.float32)
        epsilon = jnp.zeros((), dtype=jnp.float32)
        W1 = jax.random.normal(ks[2], (D, H), dtype=jnp.float32) * (1.0 / np.sqrt(D))
        b1 = jnp.zeros((H,), dtype=jnp.float32)
        rms_weight = jnp.ones((H,), dtype=jnp.float32)
        W2 = jax.random.normal(ks[3], (H, D), dtype=jnp.float32) * (1.0 / np.sqrt(H))
        b2 = jnp.zeros((D,), dtype=jnp.float32)
        return {'x': x, 'adjacency': adjacency, 'epsilon': epsilon, 'W1': W1, 'b1': b1, 'rms_weight': rms_weight, 'W2': W2, 'b2': b2}
    _L0_gnn_all = _L0_gnn_setup()
    _L0_gnn_in = {k: v for k, v in _L0_gnn_all.items() if k in ('epsilon', 'W1', 'b1', 'rms_weight', 'W2', 'b2')}
    del _L0_gnn_all

    def _L1_gnn_setup():
        import jax, jax.numpy as jnp
        import numpy as np
        B, N, C_IN, C_OUT = (8, 1024, 128, 128)
        key = jax.random.key(seed)
        k1, k2, k3 = jax.random.split(key, 3)
        x = jax.random.normal(k1, (B, N, C_IN), dtype=jnp.float32)
        adj = jax.random.uniform(k2, (B, N, N), dtype=jnp.float32)
        limit = float(np.sqrt(6.0 / (C_IN + C_OUT)))
        weight = jax.random.uniform(k3, (C_IN, C_OUT), minval=-limit, maxval=limit, dtype=jnp.float32)
        bias = jnp.zeros((C_OUT,), dtype=jnp.float32)
        return {'x': x, 'adj': adj, 'weight': weight, 'bias': bias}
    _L1_gnn_all = _L1_gnn_setup()
    _L1_gnn_in = {k: v for k, v in _L1_gnn_all.items() if k in ('weight', 'bias')}
    del _L1_gnn_all

    def _L2_gnn_setup():
        import jax, jax.numpy as jnp
        import numpy as np
        GROUPS = [list(range(25)), [0, 1, 2, 3, 4, 5, 6, 7, 8], [0, 9, 10, 11, 12, 13, 14], [6, 7, 8, 12, 13, 14], [3, 4, 5, 9, 10, 11]]
        B, N, D_IN, D_HID = (4096, 25, 128, 256)

        def _graph_conv(x, adj, W, b):
            n = adj.shape[-1]
            A = adj + jnp.eye(n, dtype=adj.dtype)
            deg = jnp.sum(A, axis=-1)
            deg_safe = jnp.where(deg == 0, 1.0, deg)
            dinv = jnp.where(deg == 0, 0.0, deg_safe ** (-0.5))
            norm_adj = dinv[:, :, None] * A * dinv[:, None, :]
            support = jnp.einsum('bnd,de->bne', x, W)
            out = jnp.einsum('bnm,bme->bne', norm_adj, support) + b
            return jax.nn.relu(out)
        key = jax.random.key(seed)
        ks = jax.random.split(key, 7)
        s1 = float(np.sqrt(6.0 / (D_IN + D_HID)))
        s2 = float(np.sqrt(6.0 / (D_HID + D_IN)))
        return {'x': jax.random.normal(ks[0], (B, N, D_IN), dtype=jnp.float32), 'adj': jax.random.uniform(ks[1], (B, N, N), dtype=jnp.float32), 'W1': jax.random.uniform(ks[2], (5, D_IN, D_HID), jnp.float32, -s1, s1), 'b1': jnp.zeros((5, D_HID), dtype=jnp.float32), 'W2': jax.random.uniform(ks[3], (5, D_HID, D_IN), jnp.float32, -s2, s2), 'b2': jnp.zeros((5, D_IN), dtype=jnp.float32), 'fusion_w': jnp.ones((5,), dtype=jnp.float32)}
    _L2_gnn_all = _L2_gnn_setup()
    _L2_gnn_in = {k: v for k, v in _L2_gnn_all.items() if k in ('W1', 'b1', 'W2', 'b2', 'fusion_w')}
    del _L2_gnn_all

    def _L3_gnn_setup():
        import jax, jax.numpy as jnp
        import numpy as np
        LN_EPS = 1e-05
        key = jax.random.key(seed)
        k1, k2, k3, k4 = jax.random.split(key, 4)
        B, N, F, O = (8, 1024, 128, 128)
        x = jax.random.normal(k1, (B, N, F), dtype=jnp.float32)
        adj = jax.random.uniform(k2, (B, N, N), dtype=jnp.float32)
        gamma = jnp.ones((F,), jnp.float32)
        beta = jnp.zeros((F,), jnp.float32)
        W_self = jax.random.normal(k3, (F, O), dtype=jnp.float32) * (1.0 / np.sqrt(F))
        W_neigh = jax.random.normal(k4, (F, O), dtype=jnp.float32) * (1.0 / np.sqrt(F))
        return {'x': x, 'adj': adj, 'gamma': gamma, 'beta': beta, 'W_self': W_self, 'W_neigh': W_neigh}
    _L3_gnn_all = _L3_gnn_setup()
    _L3_gnn_in = {k: v for k, v in _L3_gnn_all.items() if k in ('gamma', 'beta', 'W_self', 'W_neigh')}
    del _L3_gnn_all
    return {'x': x, 'adj': adj, 'L0_gnn_epsilon': _L0_gnn_in['epsilon'], 'L0_gnn_W1': _L0_gnn_in['W1'], 'L0_gnn_b1': _L0_gnn_in['b1'], 'L0_gnn_rms_weight': _L0_gnn_in['rms_weight'], 'L0_gnn_W2': _L0_gnn_in['W2'], 'L0_gnn_b2': _L0_gnn_in['b2'], 'L1_gnn_weight': _L1_gnn_in['weight'], 'L1_gnn_bias': _L1_gnn_in['bias'], 'L2_gnn_W1': _L2_gnn_in['W1'], 'L2_gnn_b1': _L2_gnn_in['b1'], 'L2_gnn_W2': _L2_gnn_in['W2'], 'L2_gnn_b2': _L2_gnn_in['b2'], 'L2_gnn_fusion_w': _L2_gnn_in['fusion_w'], 'L3_gnn_gamma': _L3_gnn_in['gamma'], 'L3_gnn_beta': _L3_gnn_in['beta'], 'L3_gnn_W_self': _L3_gnn_in['W_self'], 'L3_gnn_W_neigh': _L3_gnn_in['W_neigh']}

def reference(x, adj, L0_gnn_epsilon, L0_gnn_W1, L0_gnn_b1, L0_gnn_rms_weight, L0_gnn_W2, L0_gnn_b2, L1_gnn_weight, L1_gnn_bias, L2_gnn_W1, L2_gnn_b1, L2_gnn_W2, L2_gnn_b2, L2_gnn_fusion_w, L3_gnn_gamma, L3_gnn_beta, L3_gnn_W_self, L3_gnn_W_neigh):
    import jax
    import jax.numpy as jnp

    def _L0_gnn_ref(x, adjacency, epsilon, W1, b1, rms_weight, W2, b2):
        import jax, jax.numpy as jnp
        import numpy as np
        B, N, D, H = (8, 1024, 128, 512)
        RMS_EPS = 1e-06

        def _rmsnorm(h, w, eps=RMS_EPS):
            var = jnp.mean(jnp.square(h), axis=-1, keepdims=True)
            return h * jax.lax.rsqrt(var + eps) * w
        neighbor_sum = jnp.einsum('bnm,bmd->bnd', adjacency, x)
        agg = epsilon * x + neighbor_sum
        h = jnp.einsum('bnd,dh->bnh', agg, W1) + b1
        h = jax.nn.silu(_rmsnorm(h, rms_weight))
        out = jnp.einsum('bnh,hd->bnd', h, W2) + b2
        return out

    def _L1_gnn_ref(x, adj, weight, bias):
        import jax, jax.numpy as jnp
        import numpy as np
        B, N, C_IN, C_OUT = (8, 1024, 128, 128)
        d_inv_sqrt = (jnp.sum(adj, axis=-1) + 1e-05) ** (-0.5)
        adj_norm = d_inv_sqrt[..., :, None] * adj * d_inv_sqrt[..., None, :]
        support = jnp.einsum('bni,io->bno', x, weight)
        return jnp.einsum('bnm,bmo->bno', adj_norm, support) + bias

    def _L2_gnn_ref(x, adj, W1, b1, W2, b2, fusion_w):
        import jax, jax.numpy as jnp
        import numpy as np
        GROUPS = [list(range(25)), [0, 1, 2, 3, 4, 5, 6, 7, 8], [0, 9, 10, 11, 12, 13, 14], [6, 7, 8, 12, 13, 14], [3, 4, 5, 9, 10, 11]]
        B, N, D_IN, D_HID = (4096, 25, 128, 256)

        def _graph_conv(x, adj, W, b):
            n = adj.shape[-1]
            A = adj + jnp.eye(n, dtype=adj.dtype)
            deg = jnp.sum(A, axis=-1)
            deg_safe = jnp.where(deg == 0, 1.0, deg)
            dinv = jnp.where(deg == 0, 0.0, deg_safe ** (-0.5))
            norm_adj = dinv[:, :, None] * A * dinv[:, None, :]
            support = jnp.einsum('bnd,de->bne', x, W)
            out = jnp.einsum('bnm,bme->bne', norm_adj, support) + b
            return jax.nn.relu(out)
        norm_w = jax.nn.softmax(fusion_w)
        fused = jnp.zeros_like(x)
        for g, idx_list in enumerate(GROUPS):
            idx = jnp.asarray(idx_list)
            x_g = x[:, idx, :]
            adj_g = adj[:, idx][:, :, idx]
            h = _graph_conv(x_g, adj_g, W1[g], b1[g])
            out_g = _graph_conv(h, adj_g, W2[g], b2[g])
            fused = fused.at[:, idx, :].add(norm_w[g] * out_g)
        return fused

    def _L3_gnn_ref(x, adj, gamma, beta, W_self, W_neigh):
        import jax, jax.numpy as jnp
        import numpy as np
        LN_EPS = 1e-05
        mu = jnp.mean(x, axis=-1, keepdims=True)
        var = jnp.mean(jnp.square(x - mu), axis=-1, keepdims=True)
        xn = (x - mu) * jax.lax.rsqrt(var + LN_EPS) * gamma + beta
        d_out = jnp.sum(adj, axis=1)
        d_in = jnp.sum(adj, axis=2)
        s_out = jnp.where(d_out != 0, jax.lax.rsqrt(d_out), 0.0)
        s_in = jnp.where(d_in != 0, jax.lax.rsqrt(d_in), 0.0)
        A_norm = s_out[:, :, None] * adj * s_in[:, None, :]
        eye = jnp.eye(adj.shape[1], dtype=adj.dtype)
        L = eye[None, :, :] - A_norm
        neighbor = jnp.einsum('bij,bjf->bif', L, xn)
        pre = xn @ W_self + neighbor @ W_neigh
        return jax.nn.softplus(pre)
    x = _layernorm(x + _L0_gnn_ref(x, adj, L0_gnn_epsilon, L0_gnn_W1, L0_gnn_b1, L0_gnn_rms_weight, L0_gnn_W2, L0_gnn_b2), axis=-1)
    x = _layernorm(x + _L1_gnn_ref(x, adj, L1_gnn_weight, L1_gnn_bias), axis=-1)
    x = _layernorm(x + _L2_gnn_ref(x, adj, L2_gnn_W1, L2_gnn_b1, L2_gnn_W2, L2_gnn_b2, L2_gnn_fusion_w), axis=-1)
    x = _layernorm(x + _L3_gnn_ref(x, adj, L3_gnn_gamma, L3_gnn_beta, L3_gnn_W_self, L3_gnn_W_neigh), axis=-1)
    return x

_drawn_inputs = setup_inputs


def setup_inputs(seed=0):
    import zlib

    import numpy as np

    out = dict(_drawn_inputs(seed))
    spreads = {'L0_gnn_b1': (0.0, 0.346),
     'L0_gnn_rms_weight': (1.0, 0.2),
     'L0_gnn_b2': (0.0, 0.1),
     'L1_gnn_bias': (0.0, 0.1),
     'L2_gnn_b1': (0.0, 0.8),
     'L2_gnn_b2': (0.0, 2.0),
     'L2_gnn_fusion_w': (1.0, 0.6),
     'L3_gnn_gamma': (1.0, 0.2),
     'L3_gnn_beta': (0.0, 0.1)}
    factors = {'L2_gnn_W1': 3.208, 'L2_gnn_W2': 2.719}
    for name, (base, spread) in spreads.items():
        noise = np.random.default_rng([zlib.crc32(name.encode()), seed]).standard_normal(out[name].shape)
        drawn = base * np.exp(spread * noise) if base else spread * noise
        out[name] = jnp.asarray(drawn.astype(out[name].dtype))
    for name, factor in factors.items():
        out[name] = (out[name] * factor).astype(out[name].dtype)
    return out
```

```python
import numpy as np
import concourse.bass as bass
from concourse import mybir
from contextlib import ExitStack

GRAPHS, NODES, D, HID = 16, 512, 128, 512
P = 128
NB = NODES // P
HB = HID // P
PAIRS = GRAPHS // 2
JOINTS, NG, HID2 = 25, 5, 256
HB2 = HID2 // P
GI = NG * JOINTS
GROUPS = [list(range(25)), [0, 1, 2, 3, 4, 5, 6, 7, 8], [0, 9, 10, 11, 12, 13, 14],
          [6, 7, 8, 12, 13, 14], [3, 4, 5, 9, 10, 11]]
LN_EPS, RMS_EPS, DEG_EPS = 1e-5, 1e-6, 1e-5


def constant_columns():
    at, out = 0, {}
    for name, width in [("ident", P), ("spread", GI), ("gather", P), ("block", GI), ("member", JOINTS),
                        ("select", P), ("group", NG), ("own", 1)]:
        out[name] = (at, width)
        at += width
    return out, at


def shape_constants():
    cols, width = constant_columns()
    c = np.zeros((P, width), np.float32)

    def part(name):
        a, w = cols[name]
        return c[:, a:a + w]

    part("ident")[:] = np.eye(P)
    for g, idx in enumerate(GROUPS):
        for i in range(JOINTS):
            r = g * JOINTS + i
            part("spread")[i, r] = 1.0
            part("gather")[r, i] = 1.0
            part("block")[r, g * JOINTS:(g + 1) * JOINTS] = 1.0
            part("member")[r, idx] = 1.0
            part("group")[r, g] = 1.0
            if i in idx:
                part("select")[r, i] = 1.0
                part("own")[r, 0] = 1.0
    return c


def build(nc, x, adj, l0_eps, l0_w1, l0_b1, l0_rms, l0_w2, l0_b2, l1_w, l1_b, l2_w1, l2_b1, l2_w2,
          l2_b2, l2_fusion, l3_gamma, l3_beta, l3_self, l3_neigh, consts, out):
    fp32 = mybir.dt.float32
    ALU = mybir.AluOpType
    ACT = mybir.ActivationFunctionType
    AX = mybir.AxisListType
    cols, cwidth = constant_columns()

    ctx = ExitStack()
    with ctx:
        def sb(name, shape):
            return ctx.enter_context(nc.sbuf_tensor(name, shape, fp32))

        def sem(name):
            return ctx.enter_context(nc.semaphore(name))

        con = sb("con", [P, cwidth])
        w1 = sb("w1", [P, HID])
        w2 = sb("w2", [P, HB, D])
        b1c = sb("b1c", [P, HB])
        rmsc = sb("rmsc", [P, HB])
        b2c = sb("b2c", [P, 1])
        epsc = sb("epsc", [P, 1])
        wl1 = sb("wl1", [P, D])
        bl1 = sb("bl1", [P, D])
        gw1 = sb("gw1", [P, NG, HID2])
        gb1 = sb("gb1", [P, HB2, NG])
        ones = sb("ones", [P, 1])
        gw2 = sb("gw2", [P, NG, HB2, D])
        gb2 = sb("gb2", [P, D])
        fus = sb("fus", [P, 6 * NG])
        gammac = sb("gammac", [P, 1])
        betac = sb("betac", [P, 1])
        wself = sb("wself", [P, D])
        wneigh = sb("wneigh", [P, D])
        wsum = sb("wsum", [P, D])
        selw = sb("selw", [P, P])
        half = sb("half", [P, 24])
        ln_eps = sb("ln_eps", [P, 2 * NB])
        deg_eps = sb("deg_eps", [P, 2 * NB])
        zeros = sb("zeros", [P, 4 * NB])
        unit = sb("unit", [P, 2 * NB])
        spare = sb("spare", [1, 8])

        def const(name, rows=P):
            a, w = cols[name]
            return con[0:rows, a:a + w]

        ident = const("ident")

        def per(name, shape):
            return [[sb(f"{name}_{q}{s}", shape) for s in range(2)] for q in range(2)]

        def two(name, shape):
            return [sb(f"{name}_{s}", shape) for s in range(2)]

        adjn = two("adjn", [P, NB, NODES])
        adjT = per("adjT", [P, NB, NODES])
        xin = per("xin", [P, NB, D])
        x1b = per("x1b", [P, NB, D])
        x1s = per("x1s", [P, NB, D])
        ahatT = per("ahatT", [P, GI])
        ahatA = per("ahatA", [P, GI])
        sums = [sb(f"sums_{q}", [P, 2, 2, NB]) for q in range(2)]
        scal = [sb(f"scal_{q}", [P, 3, 2, NB]) for q in range(2)]
        ex = two("ex", [P, NB, D])
        aggT = two("aggT", [P, NODES])
        hT = two("hT", [P, HB, NODES])
        sqT = two("sqT", [P, HB, NODES])
        ssq = two("ssq", [P, NB])
        rms = two("rms", [P, NB])
        outT = two("outT", [P, NODES])
        r0 = two("r0", [P, NB, D])
        st0 = two("st0", [P, NB, 6])
        mv0 = two("mv0", [P, NB, 2])
        rs0 = two("rs0", [P, NB])
        x1 = two("x1", [P, NB, D])
        zer = sb("zer", [P, 2, 2, NB])
        zr = sb("zr", [P, 2, 2, NB])
        pw = sb("pw", [P, 3, 2, NB])
        deg = sb("deg", [P, 2])
        degz = sb("degz", [P, 6])
        dinv = sb("dinv", [P, 2])
        degj = two("degj", [P, JOINTS])
        bd = two("bd", [P, GI])
        yT = two("yT", [P, NODES])
        r1 = two("r1", [P, NB, D])
        st1 = two("st1", [P, NB, 6])
        mv1 = sb("mv1", [P, 2, NB, 2])
        vE = sb("vE", [P, 2, NB])
        rA = sb("rA", [P, 2, NB])
        vB = sb("vB", [P, 2, NB])
        tB = sb("tB", [P, 2, NB])
        rB = sb("rB", [P, 2, NB])
        rAB = sb("rAB", [P, 2, NB])
        vC = sb("vC", [P, 2, NB])
        rC = sb("rC", [P, 2, NB])
        x2 = two("x2", [P, D])
        ygT = sb("ygT", [P, 2, NG, JOINTS])
        hg = sb("hg", [P, HB2, NG, 2 * JOINTS])
        vgT = sb("vgT", [P, 2, NG, JOINTS])
        vg = sb("vg", [P, 2, D])
        og = sb("og", [P, 2, D])
        st2 = two("st2", [P, 6])
        mv2 = sb("mv2", [P, 2, 2])
        x3 = two("x3", [P, NB, D])
        xh = two("xh", [P, NB, D])
        xnT = two("xnT", [P, NODES])
        vs = two("vs", [P, NB, D])
        zT = two("zT", [P, NODES])
        tz = xh
        pre = two("pre", [P, NB, D])
        sp_abs = vs
        r3 = pre
        st3 = two("st3", [P, NB, 6])
        mv3 = two("mv3", [P, NB, 2])
        rs3 = two("rs3", [P, NB])
        yout = two("yout", [P, NB, D])

        bank = [ctx.enter_context(nc.psum_tensor(f"bank{i}", [P, 512], fp32)) for i in range(8)]

        def blocks(ap):
            return ap.rearrange("p (k n) -> p k n", k=NB)

        def flat4(tile):
            return tile[:, :, :, :].rearrange("p a s k -> p (a s k)")

        def wide(ap):
            return ap.rearrange("p k n -> p (k n)")

        weights_in = sem("weights_in")
        adj_in = [[sem(f"adj_in_{q}{s}") for s in range(2)] for q in range(2)]
        x_in = [[sem(f"x_in_{q}{s}") for s in range(2)] for q in range(2)]
        y_out = [sem(f"y_out_{s}") for s in range(2)]
        tr_ps = sem("tr_ps")
        agg_ps = sem("agg_ps")
        deg_ps = sem("deg_ps")
        bdT_ps = sem("bdT_ps")
        ahA_ps = sem("ahA_ps")
        hid_ps = sem("hid_ps")
        ssq_ps = sem("ssq_ps")
        rms_ps = sem("rms_ps")
        w2_ps = sem("w2_ps")
        o0_ps = sem("o0_ps")
        y_ps = sem("y_ps")
        o1_ps = sem("o1_ps")
        yg_ps = sem("yg_ps")
        hg_ps = sem("hg_ps")
        vgT_ps = sem("vgT_ps")
        vg_ps = sem("vg_ps")
        og_ps = sem("og_ps")
        fused_ps = sem("fused_ps")
        xhT_ps = sem("xhT_ps")
        v_ps = sem("v_ps")
        z_ps = sem("z_ps")
        zb_ps = sem("zb_ps")
        self_ps = sem("self_ps")
        adjT_sb = sem("adjT_sb")
        yT_sb = sem("yT_sb")
        aggT_sb = sem("aggT_sb")
        hid_sb = sem("hid_sb")
        sq_sb = sem("sq_sb")
        silu_sb = sem("silu_sb")
        outT_sb = sem("outT_sb")
        ygT_sb = sem("ygT_sb")
        vgT_sb = sem("vgT_sb")
        vg_sb = sem("vg_sb")
        xnT_sb = sem("xnT_sb")
        zT_sb = sem("zT_sb")
        act_abs = sem("act_abs")
        act_exp = sem("act_exp")
        act_ln = sem("act_ln")
        fus_exp = sem("fus_exp")
        setup_dve = sem("setup_dve")
        rowsum_sb = sem("rowsum_sb")
        r1_sb = sem("r1_sb")
        st1_sb = sem("st1_sb")
        mv1_sb = sem("mv1_sb")
        x2_sb = sem("x2_sb")
        deg_sb = sem("deg_sb")
        deg0_sb = sem("deg0_sb")
        sum0_sb = sem("sum0_sb")
        bd_sb = sem("bd_sb")
        ahT_sb = sem("ahT_sb")
        ahA_sb = sem("ahA_sb")
        ssq_sb = sem("ssq_sb")
        hgb_sb = sem("hgb_sb")
        hg_sb = sem("hg_sb")
        norm_sb = sem("norm_sb")
        ogb_sb = sem("ogb_sb")
        og_sb = sem("og_sb")
        r2_sb = sem("r2_sb")
        st2_sb = sem("st2_sb")
        mv2_sb = sem("mv2_sb")
        x3_sb = sem("x3_sb")
        xh_sb = sem("xh_sb")
        r0_sb = sem("r0_sb")
        st0_sb = sem("st0_sb")
        mv0_sb = sem("mv0_sb")
        x1_sb = sem("x1_sb")
        x1s_sb = sem("x1s_sb")
        vs_sb = sem("vs_sb")
        tz_sb = sem("tz_sb")
        pre_sb = sem("pre_sb")
        sp_sb = sem("sp_sb")
        r3_sb = sem("r3_sb")
        st3_sb = sem("st3_sb")
        mv3_sb = sem("mv3_sb")
        y_sb = sem("y_sb")
        half_sb = sem("half_sb")
        stat_sb = sem("stat_sb")
        rA_sb = sem("rA_sb")
        rB_sb = sem("rB_sb")
        dinv_sb = sem("dinv_sb")
        rs0_sb = sem("rs0_sb")
        rs3_sb = sem("rs3_sb")
        ex_sb = sem("ex_sb")
        sqsum = sem("sqsum")
        rms_sb = sem("rms_sb")
        ppA = sem("ppA")
        ppB = sem("ppB")
        ppD = sem("ppD")
        ppE = sem("ppE")
        ppF = sem("ppF")
        ppG = sem("ppG")
        ppH = sem("ppH")
        pp3 = sem("pp3")
        x1b_sb = sem("x1b_sb")

        N_LOADS = 15 + 3 * NG
        SETUP = 9
        block = ctx.enter_context(nc.Block())

        def take_wait(n):
            nc.vector.memset(spare[:, n:n + 1], 0.0)

        def pairs_of(engine, body):
            body(0, 0, 0, True, False)
            body(1, 0, 1, True, True)
            with engine.Fori(0, (PAIRS - 2) // 2, 1) as i:
                body(2 * i + 2, i + 1, 0, True, True)
                body(2 * i + 3, i + 1, 1, True, True)
            body(PAIRS, PAIRS // 2, 0, False, True)

        @block.sync
        def _(sp):
            loads = [(w1[:, :], l0_w1), (w2[:, :, :], l0_w2.rearrange("(k p) d -> p k d", p=P)),
                     (con[:, :], consts),
                     (wl1[:, :], l1_w), (wself[:, :], l3_self), (wneigh[:, :], l3_neigh),
                     (gw1[:, :, :], l2_w1.rearrange("g d h -> d g h")),
                     (bl1[:, :], l1_b.rearrange("(o d) -> o d", o=1).to_broadcast([P, D])),
                     (epsc[:, :], l0_eps.rearrange("(o d) -> o d", o=1).to_broadcast([P, 1])),
                     (fus[:, 0:NG], l2_fusion.rearrange("(o d) -> o d", o=1).to_broadcast([P, NG])),
                     (b2c[:, :], l0_b2.rearrange("(p o) -> p o", o=1)),
                     (gammac[:, :], l3_gamma.rearrange("(p o) -> p o", o=1)),
                     (betac[:, :], l3_beta.rearrange("(p o) -> p o", o=1)),
                     (b1c[:, :], l0_b1.rearrange("(k p) -> p k", p=P)),
                     (rmsc[:, :], l0_rms.rearrange("(k p) -> p k", p=P))]
            for g in range(NG):
                loads.append((gw2[:, g, :, :], l2_w2[g, :, :].rearrange("(k p) d -> p k d", p=P)))
                loads.append((gb1[:, :, g], l2_b1[g, :].rearrange("(k p) -> p k", p=P)))
                loads.append((gb2[g * JOINTS:(g + 1) * JOINTS, :], l2_b2[g:g + 1, :].to_broadcast([JOINTS, D])))
            assert len(loads) == N_LOADS

            def graph(tensor, g):
                if isinstance(g, int):
                    return tensor[g, :, :].rearrange("(k p) m -> p k m", p=P)
                return tensor[bass.ds(g, 1), :, :].rearrange("o (k p) m -> p (o k) m", p=P)

            def load(q, s, g):
                sp.dma_start(adjn[s][:, :, :], graph(adj, g)).then_inc(adj_in[q][s], 16)
                sp.dma_start(xin[q][s][:, :, :], graph(x, g)).then_inc(x_in[q][s], 16)

            load(0, 0, 0)
            for dst, src in loads[:3]:
                sp.dma_start(dst, src).then_inc(weights_in, 16)
            load(0, 1, 1)
            with nc.allow_non_contiguous_dma(reason="vectors of at most 512 values, once"):
                for dst, src in loads[3:]:
                    sp.dma_start(dst, src).then_inc(weights_in, 16)
            sp.wait_ge(ahA_sb, 1)
            for s in range(2):
                load(1, s, 2 + s)

            def store(g, pair, s):
                sp.wait_ge(y_sb, 4 * (2 * pair + s + 1))
                sp.dma_start(graph(out, g), yout[s][:, :, :]).then_inc(y_out[s], 16)

            def load_and_store(t, q):
                graphs = [sp.snap(2 * t + k) for k in (0, 1, -4, -3)]
                sp.wait_ge(ahA_sb, t)
                for s in range(2):
                    load(q, s, graphs[s])
                for s in range(2):
                    store(graphs[2 + s], t - 2, s)

            with sp.Fori(0, (PAIRS - 2) // 2, 1) as i:
                load_and_store(2 * i + 2, 0)
                load_and_store(2 * i + 3, 1)
            for pair in (PAIRS - 2, PAIRS - 1):
                for s in range(2):
                    store(2 * pair + s, pair, s)
            for s in range(2):
                sp.wait_ge(y_out[s], 16 * PAIRS)

        @block.tensor
        def _(pe):
            mm = nc.tensor.matmul
            tp = nc.tensor.transpose
            pe.wait_ge(weights_in, 16 * N_LOADS)
            pe.wait_ge(setup_dve, SETUP)

            def body(t, h, q, one, two_):
                u = t - 1
                def a(s):
                    return 2 * t + s + 1

                def c(s):
                    return 2 * u + s + 1
                r = 1 - q

                for s in range(2):
                    if one:
                        pe.wait_ge(adj_in[q][s], 16 * h + 16)
                    if two_:
                        pe.wait_ge(x1s_sb, c(s))
                    for j in range(NB):
                        if one:
                            n = 4 * (2 * t + s) + j
                            if s or j >= 2:
                                pe.wait_ge(adjT_sb, n - 1)
                            elif two_:
                                pe.wait_ge(*((outT_sb, 2 * t - 1) if j == 0 else (r0_sb, 2 * t)))
                            for i in range(NB):
                                last = tp(bank[j % 2][:, i * P:(i + 1) * P],
                                          adjn[s][:, i, j * P:(j + 1) * P], ident)
                            last.then_inc(tr_ps, 1)
                        if two_:
                            if j == 0:
                                if s == 0:
                                    guard_prev(pe, pre_sb, t, 2)
                                else:
                                    guard_prev(pe, tz_sb, t, 1)
                            last = mm(bank[5 + s][:, :], x1s[r][s][:, j, :], adjT[r][s][:, j, :],
                                      start=(j == 0), stop=(j == NB - 1))
                            if j == NB - 1:
                                last.then_inc(y_ps, 1)

                for s in range(2):
                    if one:
                        pe.wait_ge(adjT_sb, 4 * a(s))
                        pe.wait_ge(x_in[q][s], 16 * h + 16)
                        pe.wait_ge(ex_sb, a(s))
                        if s == 0 and two_:
                            pe.wait_ge(outT_sb, 2 * t)
                        b = bank[4 if s == 0 else 0]
                        for j in range(NB):
                            mm(b[:, :], xin[q][s][:, j, :], adjT[q][s][:, j, :], start=(j == 0), stop=False)
                        for j in range(NB):
                            last = mm(b[:, j * P:(j + 1) * P], ex[s][:, j, :], ident, start=False,
                                      stop=(j == NB - 1), is_transpose=True)
                        last.then_inc(agg_ps, 1)
                    if two_:
                        pe.wait_ge(yT_sb, c(s))
                        if s == 0:
                            guard_prev(pe, tz_sb, t, 2)
                        b = bank[7 if s == 0 else 5]
                        for i in range(NB):
                            last = mm(b[:, i * P:(i + 1) * P], yT[s][:, i * P:(i + 1) * P], wl1[:, :],
                                      start=True, stop=True)
                        last.then_inc(o1_ps, 1)

                if one:
                    for s in range(2):
                        o = bank[1][0:GI, 32 * s:32 * s + JOINTS]
                        mm(o, const("spread"), adjn[s][:, 0, 0:JOINTS], start=True, stop=False)
                        last = mm(o, const("spread"), ident[:, 0:JOINTS], start=False, stop=True)
                    last.then_inc(deg_ps, 1)
                    for s in range(2):
                        hidden(pe, s, a(s), t, two_)
                        if s == 0:
                            pe.wait_ge(bd_sb, t + 1)
                            pe.wait_ge(aggT_sb, a(1))
                            for g in range(2):
                                last = tp(bank[0][0:GI, P * g:P * g + GI], bd[g][0:GI, :], ident[0:GI, 0:GI])
                            last.then_inc(bdT_ps, 1)
                    pe.wait_ge(ahT_sb, t + 1)
                    for g in range(2):
                        last = mm(bank[1][:, P * g:P * g + GI], const("gather", GI), ahatT[q][g][0:GI, :],
                                  start=True, stop=True)
                    last.then_inc(ahA_ps, 1)
                if two_:
                    pe.wait_ge(x2_sb, c(1))
                    for s in range(2):
                        last = mm(bank[6][:, s * GI:(s + 1) * GI], x2[s][:, :], ahatA[r][s][:, :],
                                  start=True, stop=True)
                    last.then_inc(yg_ps, 1)
                if one:
                    sum_squares(pe, 0, a(0), t, two_)
                if two_:
                    pe.wait_ge(ygT_sb, u + 1)
                    for k in range(HB2):
                        for g in range(NG):
                            at = (k * NG + g) * 2 * JOINTS
                            last = mm(bank[5][:, at:at + 2 * JOINTS], gw1[:, g, k * P:(k + 1) * P],
                                      ygT[:, :, g, :], start=True, stop=True)
                    last.then_inc(hg_ps, 1)
                if one:
                    spread_rms(pe, 0, a(0), t + 1)
                if two_:
                    pe.wait_ge(hg_sb, u + 1)
                    for g in range(NG):
                        at = g * 2 * JOINTS
                        for k in range(HB2):
                            last = mm(bank[6][:, at:at + 2 * JOINTS], gw2[:, g, k, :], hg[:, k, g, :],
                                      start=(k == 0), stop=(k == HB2 - 1))
                    last.then_inc(vgT_ps, 1)
                    pe.wait_ge(vgT_sb, u + 1)
                    for s in range(2):
                        last = tp(bank[5][0:GI, s * D:(s + 1) * D], vgT[:, s, :, :].rearrange("p g i -> p (g i)"), ident)
                    last.then_inc(vg_ps, 1)
                    pe.wait_ge(vg_sb, u + 1)
                    for s in range(2):
                        last = mm(bank[6][0:GI, s * D:(s + 1) * D], ahatT[r][s][0:GI, :], vg[0:GI, s, :],
                                  start=True, stop=True)
                    last.then_inc(og_ps, 1)
                if one:
                    project_out(pe, 0, a(0))
                if two_:
                    pe.wait_ge(og_sb, u + 1)
                    mm(bank[5][:, 0:2 * D], selw[0:GI, :], wide(og[0:GI, :, :]), start=True, stop=True).then_inc(fused_ps, 1)
                if one:
                    sum_squares(pe, 1, a(1), t, two_)
                    spread_rms(pe, 1, a(1), t + 1)
                    back_to_rows(pe, 0, a(0))
                    project_out(pe, 1, a(1))
                if two_:
                    for s in range(2):
                        pe.wait_ge(xh_sb, c(s))
                        for i in range(NB):
                            last = tp(bank[6 + s][:, i * P:(i + 1) * P], xh[s][:, i, :], ident)
                        last.then_inc(xhT_ps, 1)
                    for s in range(2):
                        pe.wait_ge(xnT_sb, c(s))
                        if s == 0:
                            pe.wait_ge(r2_sb, c(1))
                        for i in range(NB):
                            last = mm(bank[5 + s][:, i * P:(i + 1) * P], xnT[s][:, i * P:(i + 1) * P],
                                      wneigh[:, :], start=True, stop=True)
                        last.then_inc(v_ps, 1)
                    for s in range(2):
                        pe.wait_ge(vs_sb, c(s))
                        if s == 0:
                            pe.wait_ge(xnT_sb, c(1))
                        b = bank[7 if s == 0 else 5]
                        for j in range(NB):
                            last = mm(b[:, :], vs[s][:, j, :], adjT[r][s][:, j, :], start=(j == 0), stop=(j == NB - 1))
                        last.then_inc(z_ps, 1)
                        if s == 0 and one:
                            back_to_rows(pe, 1, a(1))
                    for s in range(2):
                        pe.wait_ge(zT_sb, c(s))
                        if s == 0:
                            pe.wait_ge(vs_sb, c(1))
                        else:
                            pe.wait_ge(pre_sb, c(0))
                        b = bank[6 + s]
                        for i in range(NB):
                            last = tp(b[:, i * P:(i + 1) * P], zT[s][:, i * P:(i + 1) * P], ident)
                        last.then_inc(zb_ps, 1)
                        b = bank[7 if s == 0 else 5]
                        if s == 0:
                            pe.wait_ge(zT_sb, c(0))
                        else:
                            pe.wait_ge(zT_sb, c(1))
                        for i in range(NB):
                            last = mm(b[:, i * P:(i + 1) * P], xnT[s][:, i * P:(i + 1) * P], wsum[:, :],
                                      start=True, stop=True)
                        last.then_inc(self_ps, 1)
                elif one:
                    back_to_rows(pe, 1, a(1))

            def guard_prev(eng, what, t, k):
                if isinstance(t, int) and t == 1:
                    return
                eng.wait_ge(what, 2 * t - 4 + k)

            def hidden(pe, s, done, t, two_):
                pe.wait_ge(aggT_sb, done)
                for k in range(HB):
                    if not (isinstance(t, int) and t == 0 and s == 0 and k < 2):
                        pe.wait_ge(sq_sb, 4 * done - 4 + k - 1)
                    mm(bank[2 + k % 2][:, :], w1[:, k * P:(k + 1) * P], aggT[s][:, :],
                       start=True, stop=True).then_inc(hid_ps, 1)

            def sum_squares(pe, s, done, t, two_):
                pe.wait_ge(sqsum, 3 * done)
                if s:
                    pe.wait_ge(ssq_sb, done - 1)
                for i in range(NB):
                    last = mm(bank[4][:, 2 * i:2 * i + 1], sqT[s][:, 0, i * P:(i + 1) * P], ones[:, :],
                              start=True, stop=True)
                last.then_inc(ssq_ps, 1)

            def spread_rms(pe, s, done, t1):
                pe.wait_ge(rms_sb, done)
                if s == 0:
                    pe.wait_ge(ahA_sb, t1)
                else:
                    pe.wait_ge(norm_sb, 4 * (done - 1))
                for i in range(NB):
                    last = tp(bank[1][:, i * P:(i + 1) * P], rms[s][:, i:i + 1].to_broadcast([P, P]), ident)
                last.then_inc(rms_ps, 1)

            def project_out(pe, s, done):
                b = bank[0 if s == 0 else 4]
                for k in range(HB):
                    pe.wait_ge(silu_sb, 4 * done - 4 + k + 1)
                    last = mm(b[:, :], w2[:, k, :], hT[s][:, k, :], start=(k == 0), stop=(k == HB - 1))
                last.then_inc(w2_ps, 1)

            def back_to_rows(pe, s, done):
                pe.wait_ge(outT_sb, done)
                if s == 0:
                    pe.wait_ge(norm_sb, 4 * (done + 1))
                else:
                    pe.wait_ge(r0_sb, done - 1)
                for i in range(NB):
                    last = tp(bank[1][:, i * P:(i + 1) * P], outT[s][:, i * P:(i + 1) * P], ident)
                last.then_inc(o0_ps, 1)

            pairs_of(pe, body)

        @block.scalar
        def _(act):
            A = nc.scalar.activation
            act.wait_ge(weights_in, 16 * N_LOADS)
            act.wait_ge(setup_dve, 2)
            A(fus[:, 15:20], fus[:, 10:15], ACT.Exp).then_inc(fus_exp, 1)

            def body(t, h, q, one, two_):
                u = t - 1

                def a(s):
                    return 2 * t + s + 1

                def c(s):
                    return 2 * u + s + 1

                for s in range(2):
                    if one:
                        for j in range(NB):
                            act.wait_ge(tr_ps, 4 * (2 * t + s) + j + 1)
                            A(adjT[q][s][:, j, :], bank[j % 2][:, :], ACT.Identity,
                              accum_out=sums[q][:, 1, s, j:j + 1]).then_inc(adjT_sb, 1)
                    if two_:
                        act.wait_ge(y_ps, c(s))
                        A(yT[s][:, :], bank[5 + s][:, :], ACT.Identity).then_inc(yT_sb, 1)
                if one:
                    for s in range(2):
                        act.wait_ge(agg_ps, a(s))
                        A(aggT[s][:, :], bank[4 if s == 0 else 0][:, :], ACT.Identity).then_inc(aggT_sb, 1)
                    for s in range(2):
                        for k in range(HB):
                            act.wait_ge(hid_ps, 4 * (2 * t + s) + k + 1)
                            A(hT[s][:, k, :], bank[2 + k % 2][:, :], ACT.Identity, bias=b1c[:, k:k + 1]).then_inc(hid_sb, 1)
                            A(sqT[s][:, k, :], bank[2 + k % 2][:, :], ACT.Square, bias=b1c[:, k:k + 1]).then_inc(sq_sb, 1)
                if two_:
                    act.wait_ge(yg_ps, u + 1)
                    A(ygT[:, :, :, :].rearrange("p s g i -> p (s g i)"), bank[6][:, 0:2 * GI], ACT.Identity).then_inc(ygT_sb, 1)
                    act.wait_ge(vgT_ps, u + 1)
                    A(vgT[:, :, :, :].rearrange("p s g i -> p g s i"),
                      bank[6][:, 0:2 * GI].rearrange("p (g s i) -> p g s i", g=NG, s=2), ACT.Identity).then_inc(vgT_sb, 1)
                    act.wait_ge(vg_ps, u + 1)
                    A(wide(vg[0:GI, :, :]), bank[5][0:GI, 0:2 * D], ACT.Identity).then_inc(vg_sb, 1)

                def silu(s):
                    for k in range(HB):
                        act.wait_ge(norm_sb, 4 * (2 * t + s) + k + 1)
                        A(hT[s][:, k, :], hT[s][:, k, :], ACT.Silu, scale=rmsc[:, k:k + 1]).then_inc(silu_sb, 1)

                def l0_out(s):
                    act.wait_ge(w2_ps, a(s))
                    A(outT[s][:, :], bank[0 if s == 0 else 4][:, :], ACT.Identity, bias=b2c[:, 0:1]).then_inc(outT_sb, 1)

                if one:
                    silu(0)
                    l0_out(0)
                    silu(1)
                if two_:
                    for s in range(2):
                        act.wait_ge(xhT_ps, c(s))
                        A(xnT[s][:, :], bank[6 + s][:, :], ACT.Identity, bias=betac[:, 0:1],
                          scale=gammac[:, 0:1]).then_inc(xnT_sb, 1)
                if one:
                    l0_out(1)
                if two_:
                    for s in range(2):
                        act.wait_ge(z_ps, c(s))
                        A(zT[s][:, :], bank[7 if s == 0 else 5][:, :], ACT.Identity).then_inc(zT_sb, 1)
                    for s in range(2):
                        act.wait_ge(pre_sb, c(s))
                        e = wide(sp_abs[s][:, :, :])
                        A(e, wide(pre[s][:, :, :]), ACT.Abs).then_inc(act_abs, 1)
                        act.wait_ge(act_abs, c(s))
                        A(e, e, ACT.Exp, scale=-1.0).then_inc(act_exp, 1)
                        act.wait_ge(act_exp, c(s))
                        A(e, e, ACT.Ln, bias=1.0).then_inc(act_ln, 1)

            pairs_of(act, body)

        @block.vector
        def _(dve):
            V = nc.vector

            dve.wait_ge(weights_in, 16 * N_LOADS)
            V.reduce_max(fus[:, 5:6], fus[:, 0:NG], AX.X).then_inc(setup_dve, 1)
            dve.wait_ge(setup_dve, 1)
            V.tensor_scalar(fus[:, 10:15], fus[:, 0:NG], fus[:, 5:6], None, ALU.subtract).then_inc(setup_dve, 1)
            V.tensor_tensor(wsum[:, :], wself[:, :], wneigh[:, :], ALU.add).then_inc(setup_dve, 1)
            V.memset(ones[:, :], 1.0).then_inc(setup_dve, 1)
            dve.wait_ge(fus_exp, 1)
            V.tensor_reduce(fus[:, 6:7], fus[:, 15:20], AX.X, ALU.add).then_inc(setup_dve, 1)
            V.tensor_tensor(fus[:, 20:25], fus[:, 15:20], const("group"), ALU.mult).then_inc(setup_dve, 1)
            dve.wait_ge(setup_dve, 6)
            V.reciprocal(fus[:, 7:8], fus[:, 6:7]).then_inc(setup_dve, 1)
            V.tensor_reduce(fus[:, 8:9], fus[:, 20:25], AX.X, ALU.add).then_inc(setup_dve, 1)
            dve.wait_ge(setup_dve, 8)
            V.tensor_scalar(selw[:, :], const("select"), fus[:, 7:8], fus[:, 8:9], ALU.mult, ALU.mult).then_inc(setup_dve, 1)

            def body(t, h, q, one, two_):
                u = t - 1
                r = 1 - q

                def a(s):
                    return 2 * t + s + 1

                def c(s):
                    return 2 * u + s + 1

                if one:
                    for s in range(2):
                        dve.wait_ge(adj_in[q][s], 16 * h + 16)
                        V.tensor_reduce(sums[q][:, 0, s, :], adjn[s][:, :, :], AX.X, ALU.add).then_inc(rowsum_sb, 1)
                if two_:
                    for s in range(2):
                        dve.wait_ge(o1_ps, c(s))
                        dve.wait_ge(x1b_sb, c(s))
                        for i in range(NB):
                            last = V.scalar_tensor_tensor(
                                out=r1[s][:, i, :], in0=bank[7 if s == 0 else 5][:, i * P:(i + 1) * P],
                                scalar=scal[r][:, 0, s, i:i + 1], in1=x1b[r][s][:, i, :], op0=ALU.mult, op1=ALU.add)
                        last.then_inc(r1_sb, 1)
                    for s in range(2):
                        dve.wait_ge(r1_sb, c(s))
                        for i in range(NB):
                            last = V.bn_stats(st1[s][:, i, :], r1[s][:, i, :])
                        last.then_inc(st1_sb, 1)
                    for s in range(2):
                        dve.wait_ge(st1_sb, c(s))
                        take_wait(s)
                        for i in range(NB):
                            last = V.bn_aggr(mv1[:, s, i, :], st1[s][:, i, :])
                        last.then_inc(mv1_sb, 1)
                if one:
                    dve.wait_ge(deg_ps, t + 1)
                    for s in range(2):
                        V.tensor_tensor_reduce(out=degj[s][0:GI, :], in0=bank[1][0:GI, 32 * s:32 * s + JOINTS],
                                               in1=const("member", GI), scale=1.0, scalar=0.0, op0=ALU.mult,
                                               op1=ALU.add, accum_out=deg[0:GI, s:s + 1]).then_inc(deg_sb, 1)
                    dve.wait_ge(deg_sb, 2 * t + 2)
                    V.tensor_scalar(degz[0:GI, 0:2], deg[0:GI, :], 0.0, None, ALU.is_equal).then_inc(deg0_sb, 1)
                if two_:
                    for s in range(2):
                        dve.wait_ge(rA_sb, u + 1)
                        dve.wait_ge(mv1_sb, c(s))
                        V.tensor_scalar(x2[s][:, :], r1[s][:, 0, :], mv1[:, s, 0, 0:1], rA[:, s, 0:1],
                                        ALU.subtract, ALU.mult).then_inc(x2_sb, 1)
                if one:
                    dve.wait_ge(dinv_sb, t + 1)
                    for s in range(2):
                        last = V.scalar_tensor_tensor(
                            out=bd[s][0:GI, :].rearrange("p (g j) -> p g j", g=NG),
                            in0=bank[1][0:GI, 32 * s:32 * s + JOINTS].rearrange("p (o j) -> p o j", o=1)
                            .to_broadcast([GI, NG, JOINTS]),
                            scalar=dinv[0:GI, s:s + 1],
                            in1=const("block", GI).rearrange("p (g j) -> p g j", g=NG), op0=ALU.mult, op1=ALU.mult)
                    last.then_inc(bd_sb, 1)
                    dve.wait_ge(bdT_ps, t + 1)
                    for s in range(2):
                        last = V.tensor_scalar(ahatT[q][s][0:GI, :], bank[0][0:GI, P * s:P * s + GI],
                                               dinv[0:GI, s:s + 1], None, ALU.mult)
                    last.then_inc(ahT_sb, 1)
                    dve.wait_ge(ahA_ps, t + 1)
                    for s in range(2):
                        last = V.tensor_copy(ahatA[q][s][:, :], bank[1][:, P * s:P * s + GI])
                    last.then_inc(ahA_sb, 1)
                    dve.wait_ge(rowsum_sb, 2 * t + 2)
                    dve.wait_ge(adjT_sb, 8 * t + 8)
                    V.tensor_scalar(flat4(zer), flat4(sums[q]), 0.0, None, ALU.is_equal).then_inc(sum0_sb, 1)

                def mean_square(s):
                    dve.wait_ge(ssq_ps, a(s))
                    V.tensor_scalar(ssq[s][:, :], bank[4][:, 0:2 * NB].rearrange("p (k o) -> p k o", o=2)[:, :, 0],
                                    1.0 / HID, RMS_EPS, ALU.mult, ALU.add).then_inc(ssq_sb, 1)

                def normalise(s):
                    dve.wait_ge(rms_ps, a(s))
                    dve.wait_ge(hid_sb, 4 * a(s))
                    for k in range(HB):
                        V.tensor_tensor(hT[s][:, k, :], hT[s][:, k, :], bank[1][:, :], ALU.mult).then_inc(norm_sb, 1)

                if one:
                    mean_square(0)
                if two_:
                    dve.wait_ge(hg_ps, u + 1)
                    n = HB2 * NG
                    hflat = hg[:, :, :, :].rearrange("p k g i -> p (k g) i")
                    V.tensor_tensor(hflat, bank[5][:, 0:n * 2 * JOINTS].rearrange("p (n i) -> p n i", n=n),
                                    gb1[:, :, :].rearrange("p k (g o) -> p (k g) o", o=1).to_broadcast([P, n, 2 * JOINTS]),
                                    ALU.add).then_inc(hgb_sb, 1)
                    dve.wait_ge(hgb_sb, u + 1)
                    V.tensor_scalar(hflat, hflat, 0.0, None, ALU.max).then_inc(hg_sb, 1)
                if one:
                    normalise(0)
                if two_:
                    dve.wait_ge(og_ps, u + 1)
                    V.tensor_tensor(og[0:GI, :, :], bank[6][0:GI, 0:2 * D].rearrange("p (s d) -> p s d", s=2),
                                    gb2[0:GI, :].rearrange("p (o d) -> p o d", o=1).to_broadcast([GI, 2, D]),
                                    ALU.add).then_inc(ogb_sb, 1)
                    dve.wait_ge(ogb_sb, u + 1)
                    V.tensor_scalar(og[0:GI, :, :], og[0:GI, :, :], 0.0, None, ALU.max).then_inc(og_sb, 1)
                    dve.wait_ge(fused_ps, u + 1)
                    for s in range(2):
                        V.tensor_tensor(r1[s][:, 0, :], bank[5][:, s * D:(s + 1) * D], x2[s][:, :],
                                        ALU.add).then_inc(r2_sb, 1)
                    for s in range(2):
                        dve.wait_ge(r2_sb, c(s))
                        V.bn_stats(st2[s][:, :], r1[s][:, 0, :]).then_inc(st2_sb, 1)
                    dve.wait_ge(ppA, 3 * u + 2)
                    for s in range(2):
                        dve.wait_ge(st2_sb, c(s))
                        take_wait(2 + s)
                        V.bn_aggr(mv1[:, s, 0, :], st2[s][:, :]).then_inc(mv2_sb, 1)
                if one:
                    mean_square(1)
                    normalise(1)
                if two_:
                    dve.wait_ge(rB_sb, u + 1)
                    for s in range(2):
                        for i in range(NB):
                            last = V.tensor_scalar(x3[s][:, i, :], r1[s][:, i, :], mv1[:, s, i, 0:1], rAB[:, s, i:i + 1],
                                                   ALU.subtract, ALU.mult)
                        last.then_inc(x3_sb, 1)
                        dve.wait_ge(x3_sb, c(s))
                        V.tensor_tensor(xh[s][:, :, :], x3[s][:, :, :],
                                        rC[:, s, :].rearrange("p (k o) -> p k o", o=1).to_broadcast([P, NB, D]),
                                        ALU.mult).then_inc(xh_sb, 1)

                def l0_residual(s):
                    dve.wait_ge(o0_ps, a(s))
                    V.tensor_tensor(wide(r0[s][:, :, :]), bank[1][:, :], wide(xin[q][s][:, :, :]), ALU.add).then_inc(r0_sb, 1)
                    dve.wait_ge(r0_sb, a(s))
                    for i in range(NB):
                        last = V.bn_stats(st0[s][:, i, :], r0[s][:, i, :])
                    last.then_inc(st0_sb, 1)
                    dve.wait_ge(st0_sb, a(s))
                    take_wait(4 + s)
                    for i in range(NB):
                        last = V.bn_aggr(mv0[s][:, i, :], st0[s][:, i, :])
                    last.then_inc(mv0_sb, 1)

                def l0_norm(s):
                    dve.wait_ge(rs0_sb, a(s))
                    for i in range(NB):
                        last = V.tensor_scalar(x1[s][:, i, :], r0[s][:, i, :], mv0[s][:, i, 0:1], rs0[s][:, i:i + 1],
                                               ALU.subtract, ALU.mult)
                    last.then_inc(x1_sb, 1)
                    dve.wait_ge(x1_sb, a(s))
                    dve.wait_ge(stat_sb, t + 1)
                    V.tensor_tensor(x1s[q][s][:, :, :], x1[s][:, :, :],
                                    scal[q][:, 0, s, :].rearrange("p (k o) -> p k o", o=1).to_broadcast([P, NB, D]),
                                    ALU.mult).then_inc(x1s_sb, 1)

                if one:
                    l0_residual(0)
                if two_:
                    for s in range(2):
                        dve.wait_ge(v_ps, c(s))
                        V.tensor_tensor(vs[s][:, :, :], blocks(bank[5 + s][:, :]),
                                        scal[r][:, 1, s, :].rearrange("p (k o) -> p k o", o=1).to_broadcast([P, NB, D]),
                                        ALU.mult).then_inc(vs_sb, 1)
                if one:
                    l0_norm(0)
                    l0_residual(1)
                    l0_norm(1)
                if two_:
                    for s in range(2):
                        dve.wait_ge(zb_ps, c(s))
                        V.tensor_tensor(tz[s][:, :, :], blocks(bank[6 + s][:, :]),
                                        scal[r][:, 2, s, :].rearrange("p (k o) -> p k o", o=1).to_broadcast([P, NB, D]),
                                        ALU.mult).then_inc(tz_sb, 1)
                        dve.wait_ge(self_ps, c(s))
                        dve.wait_ge(tz_sb, c(s))
                        V.tensor_tensor(pre[s][:, :, :], blocks(bank[7 if s == 0 else 5][:, :]), tz[s][:, :, :],
                                        ALU.add).then_inc(pre_sb, 1)
                    for s in range(2):
                        dve.wait_ge(act_ln, c(s))
                        V.scalar_tensor_tensor(out=pre[s][:, :, :], in0=pre[s][:, :, :], scalar=0.0,
                                               in1=sp_abs[s][:, :, :], op0=ALU.max, op1=ALU.add).then_inc(sp_sb, 1)
                        dve.wait_ge(sp_sb, c(s))
                        V.tensor_tensor(r3[s][:, :, :], pre[s][:, :, :], x3[s][:, :, :], ALU.add).then_inc(r3_sb, 1)
                        dve.wait_ge(r3_sb, c(s))
                        for i in range(NB):
                            last = V.bn_stats(st3[s][:, i, :], r3[s][:, i, :])
                        last.then_inc(st3_sb, 1)
                        dve.wait_ge(st3_sb, c(s))
                        take_wait(6 + s)
                        for i in range(NB):
                            last = V.bn_aggr(mv3[s][:, i, :], st3[s][:, i, :])
                        last.then_inc(mv3_sb, 1)
                    for s in range(2):
                        dve.wait_ge(rs3_sb, c(s))
                        if not (isinstance(t, int) and t == 1):
                            dve.wait_ge(y_out[s], 16 * u)
                        for i in range(NB):
                            V.tensor_scalar(yout[s][:, i, :], r3[s][:, i, :], mv3[s][:, i, 0:1], rs3[s][:, i:i + 1],
                                            ALU.subtract, ALU.mult).then_inc(y_sb, 1)

            pairs_of(dve, body)

        @block.gpsimd
        def _(pool):
            G = nc.gpsimd
            for tile, value in ((half, -0.5), (ln_eps, LN_EPS), (deg_eps, DEG_EPS), (zeros, 0.0), (unit, 1.0)):
                G.memset(tile[:, :], value).then_inc(half_sb, 1)
            pool.wait_ge(weights_in, 16 * N_LOADS)
            pool.wait_ge(half_sb, 5)

            def slots(tile):
                return tile[:, 0:2 * NB].rearrange("p (s k) -> p s k", s=2)

            def rsqrt(out_, in_, n, what):
                G.tensor_tensor(out_, in_, half[0:in_.shape[0], 0:n], ALU.pow).then_inc(what, 1)

            def body(t, h, q, one, two_):
                u = t - 1

                def a(s):
                    return 2 * t + s + 1

                def c(s):
                    return 2 * u + s + 1

                if one:
                    for s in range(2):
                        pool.wait_ge(x_in[q][s], 16 * h + 16)
                        if two_:
                            pool.wait_ge(agg_ps, 2 * t - 1 + s)
                        G.tensor_tensor(wide(ex[s][:, :, :]), wide(xin[q][s][:, :, :]),
                                        epsc[:, 0:1].to_broadcast([P, NB * D]), ALU.mult).then_inc(ex_sb, 1)
                if two_:
                    pool.wait_ge(mv1_sb, c(1))
                    if not (isinstance(t, int) and t == 1):
                        pool.wait_ge(xh_sb, c(1) - 2)
                    v = mv1[:, :, :, 1]
                    G.tensor_tensor(vE[:, :, :], v, slots(ln_eps), ALU.add).then_inc(ppA, 1)
                    pool.wait_ge(ppA, 3 * u + 1)
                    rsqrt(wide(rA[:, :, :]), wide(vE[:, :, :]), 2 * NB, rA_sb)
                    pool.wait_ge(rA_sb, u + 1)
                    G.tensor_tensor(tB[:, :, :], v, rA[:, :, :], ALU.mult).then_inc(ppA, 1)
                    pool.wait_ge(ppA, 3 * u + 2)
                    G.tensor_tensor(vB[:, :, :], tB[:, :, :], rA[:, :, :], ALU.mult).then_inc(ppA, 1)
                if one:
                    pool.wait_ge(deg0_sb, t + 1)
                    d = degz[0:GI, :]
                    G.tensor_tensor(d[:, 2:4], deg[0:GI, :], d[:, 0:2], ALU.add).then_inc(ppD, 1)
                    pool.wait_ge(ppD, 3 * t + 1)
                    rsqrt(d[:, 4:6], d[:, 2:4], 2, ppD)
                    G.tensor_tensor(d[:, 0:2], unit[0:GI, 0:2], d[:, 0:2], ALU.subtract).then_inc(ppD, 1)
                    pool.wait_ge(ppD, 3 * t + 3)
                    G.tensor_tensor(d[:, 0:2], d[:, 0:2], d[:, 4:6], ALU.mult).then_inc(ppE, 1)
                    pool.wait_ge(ppE, t + 1)
                    G.tensor_tensor(dinv[0:GI, :], d[:, 0:2], const("own", GI).to_broadcast([GI, 2]), ALU.mult).then_inc(dinv_sb, 1)

                def add_squares(s):
                    n = 3 * (2 * t + s)
                    pool.wait_ge(sq_sb, 4 * (2 * t + s) + 2)
                    G.tensor_tensor(sqT[s][:, 0, :], sqT[s][:, 0, :], sqT[s][:, 1, :], ALU.add).then_inc(sqsum, 1)
                    pool.wait_ge(sq_sb, 4 * (2 * t + s) + 4)
                    G.tensor_tensor(sqT[s][:, 2, :], sqT[s][:, 2, :], sqT[s][:, 3, :], ALU.add).then_inc(sqsum, 1)
                    pool.wait_ge(sqsum, n + 2)
                    G.tensor_tensor(sqT[s][:, 0, :], sqT[s][:, 0, :], sqT[s][:, 2, :], ALU.add).then_inc(sqsum, 1)

                def inverse_rms(s):
                    pool.wait_ge(ssq_sb, a(s))
                    rsqrt(rms[s][:, :], ssq[s][:, :], NB, rms_sb)

                if one:
                    add_squares(0)
                    inverse_rms(0)
                    add_squares(1)
                if two_:
                    pool.wait_ge(mv2_sb, c(1))
                    pool.wait_ge(ppA, 3 * u + 3)
                    G.tensor_tensor(vB[:, :, 0:1], mv1[:, :, 0:1, 1], slots(zeros)[:, :, 0:1], ALU.add).then_inc(ppB, 1)
                    pool.wait_ge(ppB, 7 * u + 1)
                    G.tensor_tensor(tB[:, :, :], vB[:, :, :], slots(ln_eps), ALU.add).then_inc(ppB, 1)
                    pool.wait_ge(ppB, 7 * u + 2)
                    rsqrt(wide(rB[:, :, :]), wide(tB[:, :, :]), 2 * NB, ppB)
                    pool.wait_ge(ppB, 7 * u + 3)
                    G.tensor_tensor(rAB[:, :, :], rA[:, :, :], rB[:, :, :], ALU.mult).then_inc(ppB, 1)
                    G.tensor_tensor(vC[:, :, :], vB[:, :, :], rB[:, :, :], ALU.mult).then_inc(ppB, 1)
                    pool.wait_ge(ppB, 7 * u + 5)
                    G.tensor_tensor(rAB[:, :, 0:1], rB[:, :, 0:1], slots(zeros)[:, :, 0:1], ALU.add).then_inc(ppB, 1)
                    G.tensor_tensor(vC[:, :, :], vC[:, :, :], rB[:, :, :], ALU.mult).then_inc(ppB, 1)
                    pool.wait_ge(ppB, 7 * u + 7)
                    G.tensor_tensor(vC[:, :, :], vC[:, :, :], slots(ln_eps), ALU.add).then_inc(ppF, 1)
                    pool.wait_ge(ppF, u + 1)
                    rsqrt(wide(rC[:, :, :]), wide(vC[:, :, :]), 2 * NB, rB_sb)
                if one:
                    inverse_rms(1)
                    pool.wait_ge(sum0_sb, t + 1)
                    if two_ and not (isinstance(t, int) and t == 1):
                        pool.wait_ge(tz_sb, 2 * t - 2)
                    S = sums[q]
                    G.tensor_tensor(pw[:, 0, :, :], S[:, 0, :, :], slots(deg_eps), ALU.add).then_inc(ppG, 1)
                    pool.wait_ge(ppG, 5 * t + 1)
                    G.tensor_tensor(pw[:, 1:3, :, :], S[:, :, :, :], zer[:, :, :, :], ALU.add).then_inc(ppG, 1)
                    pool.wait_ge(ppG, 5 * t + 2)
                    G.tensor_tensor(zr[:, 0, :, :], slots(unit), zer[:, 0, :, :], ALU.subtract).then_inc(ppG, 1)
                    G.tensor_tensor(zr[:, 1, :, :], zer[:, 1, :, :], slots(unit), ALU.subtract).then_inc(ppG, 1)
                    flat = scal[q][:, :, :, :].rearrange("p a s k -> p (a s k)")
                    rsqrt(flat, pw[:, :, :, :].rearrange("p a s k -> p (a s k)"), 24, ppG)
                    pool.wait_ge(ppG, 5 * t + 5)
                    G.tensor_tensor(scal[q][:, 1:3, :, :], scal[q][:, 1:3, :, :], zr[:, :, :, :], ALU.mult).then_inc(stat_sb, 1)

                def l0_scale(s):
                    pool.wait_ge(mv0_sb, a(s))
                    G.tensor_tensor(mv0[s][:, :, 1], mv0[s][:, :, 1], ln_eps[:, 0:NB], ALU.add).then_inc(ppH, 1)
                    pool.wait_ge(ppH, a(s))
                    rsqrt(rs0[s][:, :], mv0[s][:, :, 1], NB, rs0_sb)

                def l0_bias(s):
                    pool.wait_ge(x1_sb, a(s))
                    G.tensor_tensor(x1b[q][s][:, :, :], x1[s][:, :, :],
                                    bl1[:, :].rearrange("p (o d) -> p o d", o=1).to_broadcast([P, NB, D]),
                                    ALU.add).then_inc(x1b_sb, 1)

                if one:
                    l0_scale(0)
                    l0_scale(1)
                    l0_bias(0)
                    l0_bias(1)
                if two_:
                    for s in range(2):
                        pool.wait_ge(mv3_sb, c(s))
                        G.tensor_tensor(mv3[s][:, :, 1], mv3[s][:, :, 1], ln_eps[:, 0:NB], ALU.add).then_inc(pp3, 1)
                        pool.wait_ge(pp3, c(s))
                        rsqrt(rs3[s][:, :], mv3[s][:, :, 1], NB, rs3_sb)

            pairs_of(pool, body)


INPUTS = ['x', 'adj', 'L0_gnn_epsilon', 'L0_gnn_W1', 'L0_gnn_b1', 'L0_gnn_rms_weight', 'L0_gnn_W2', 'L0_gnn_b2',
          'L1_gnn_weight', 'L1_gnn_bias', 'L2_gnn_W1', 'L2_gnn_b1', 'L2_gnn_W2', 'L2_gnn_b2', 'L2_gnn_fusion_w',
          'L3_gnn_gamma', 'L3_gnn_beta', 'L3_gnn_W_self', 'L3_gnn_W_neigh']


def kernel(**inputs):
    import concourse.bacc as bacc
    from concourse.bass_utils import run_bass_kernel_spmd

    nc = bacc.Bacc("TRN2", target_bir_lowering=False, num_devices=1)
    arrays, args = {}, []
    for name in INPUTS:
        a = np.ascontiguousarray(np.asarray(inputs[name]))
        if a.ndim == 0 or name == 'L0_gnn_epsilon':
            a = a.reshape(1)
        arrays[name] = a
    arrays["shape_constants"] = shape_constants()
    for name, a in arrays.items():
        args.append(nc.dram_tensor(name, a.shape, mybir.dt.from_np(a.dtype), kind="ExternalInput").ap())
    out = nc.dram_tensor("out", (GRAPHS, NODES, D), mybir.dt.float32, kind="ExternalOutput").ap()
    build(nc, *args, out)
    r = run_bass_kernel_spmd(nc, [arrays], core_ids=[0])
    return r.results[0]["out"]
```

```python
import numpy as np
import concourse.bass as bass
from concourse import mybir
from contextlib import ExitStack

GRAPHS, NODES, D, HID = 16, 512, 128, 512
P = 128
NB = NODES // P
HB = HID // P
PAIRS = GRAPHS // 2
JOINTS, NG, HID2 = 25, 5, 256
HB2 = HID2 // P
GI = NG * JOINTS
GROUPS = [list(range(25)), [0, 1, 2, 3, 4, 5, 6, 7, 8], [0, 9, 10, 11, 12, 13, 14],
          [6, 7, 8, 12, 13, 14], [3, 4, 5, 9, 10, 11]]
LN_EPS, RMS_EPS, DEG_EPS = 1e-5, 1e-6, 1e-5


def constant_columns():
    at, out = 0, {}
    for name, width in [("ident", P), ("spread", GI), ("gather", P), ("block", GI), ("member", JOINTS),
                        ("select", P), ("group", NG), ("own", 1)]:
        out[name] = (at, width)
        at += width
    return out, at


def shape_constants():
    cols, width = constant_columns()
    c = np.zeros((P, width), np.float32)

    def part(name):
        a, w = cols[name]
        return c[:, a:a + w]

    part("ident")[:] = np.eye(P)
    for g, idx in enumerate(GROUPS):
        for i in range(JOINTS):
            r = g * JOINTS + i
            part("spread")[i, r] = 1.0
            part("gather")[r, i] = 1.0
            part("block")[r, g * JOINTS:(g + 1) * JOINTS] = 1.0
            part("member")[r, idx] = 1.0
            part("group")[r, g] = 1.0
            if i in idx:
                part("select")[r, i] = 1.0
                part("own")[r, 0] = 1.0
    return c


def build(nc, x, adj, l0_eps, l0_w1, l0_b1, l0_rms, l0_w2, l0_b2, l1_w, l1_b, l2_w1, l2_b1, l2_w2,
          l2_b2, l2_fusion, l3_gamma, l3_beta, l3_self, l3_neigh, consts, out):
    fp32 = mybir.dt.float32
    ALU = mybir.AluOpType
    ACT = mybir.ActivationFunctionType
    AX = mybir.AxisListType
    cols, cwidth = constant_columns()

    ctx = ExitStack()
    with ctx:
        def sb(name, shape):
            return ctx.enter_context(nc.sbuf_tensor(name, shape, fp32))

        def sem(name):
            return ctx.enter_context(nc.semaphore(name))

        con = sb("con", [P, cwidth])
        w1 = sb("w1", [P, HID])
        w2 = sb("w2", [P, HB, D])
        b1c = sb("b1c", [P, HB])
        rmsc = sb("rmsc", [P, HB])
        b2c = sb("b2c", [P, 1])
        epsc = sb("epsc", [P, 1])
        wl1 = sb("wl1", [P, D])
        bl1 = sb("bl1", [P, D])
        gw1 = sb("gw1", [P, NG, HID2])
        gb1 = sb("gb1", [P, HB2, NG])
        ones = sb("ones", [P, 1])
        gw2 = sb("gw2", [P, NG, HB2, D])
        gb2 = sb("gb2", [P, D])
        fus = sb("fus", [P, 6 * NG])
        gammac = sb("gammac", [P, 1])
        betac = sb("betac", [P, 1])
        wself = sb("wself", [P, D])
        wneigh = sb("wneigh", [P, D])
        wsum = sb("wsum", [P, D])
        selw = sb("selw", [P, P])
        half = sb("half", [P, 24])
        ln_eps = sb("ln_eps", [P, 2 * NB])
        deg_eps = sb("deg_eps", [P, 2 * NB])
        zeros = sb("zeros", [P, 4 * NB])
        unit = sb("unit", [P, 2 * NB])
        spare = sb("spare", [1, 8])

        def const(name, rows=P):
            a, w = cols[name]
            return con[0:rows, a:a + w]

        ident = const("ident")

        def per(name, shape):
            return [[sb(f"{name}_{q}{s}", shape) for s in range(2)] for q in range(2)]

        def two(name, shape):
            return [sb(f"{name}_{s}", shape) for s in range(2)]

        adjn = two("adjn", [P, NB, NODES])
        adjT = per("adjT", [P, NB, NODES])
        xin = per("xin", [P, NB, D])
        x1b = per("x1b", [P, NB, D])
        x1s = per("x1s", [P, NB, D])
        ahatT = per("ahatT", [P, GI])
        ahatA = per("ahatA", [P, GI])
        sums = [sb(f"sums_{q}", [P, 2, 2, NB]) for q in range(2)]
        scal = [sb(f"scal_{q}", [P, 3, 2, NB]) for q in range(2)]
        ex = two("ex", [P, NB, D])
        aggT = two("aggT", [P, NODES])
        hT = two("hT", [P, HB, NODES])
        sqT = two("sqT", [P, HB, NODES])
        ssq = two("ssq", [P, NB])
        rms = two("rms", [P, NB])
        outT = two("outT", [P, NODES])
        r0 = two("r0", [P, NB, D])
        st0 = two("st0", [P, NB, 6])
        mv0 = two("mv0", [P, NB, 2])
        rs0 = two("rs0", [P, NB])
        x1 = two("x1", [P, NB, D])
        zer = sb("zer", [P, 2, 2, NB])
        zr = sb("zr", [P, 2, 2, NB])
        pw = sb("pw", [P, 3, 2, NB])
        deg = sb("deg", [P, 2])
        degz = sb("degz", [P, 6])
        dinv = sb("dinv", [P, 2])
        degj = two("degj", [P, JOINTS])
        bd = two("bd", [P, GI])
        yT = two("yT", [P, NODES])
        r1 = two("r1", [P, NB, D])
        st1 = two("st1", [P, NB, 6])
        mv1 = sb("mv1", [P, 2, NB, 2])
        vE = sb("vE", [P, 2, NB])
        rA = sb("rA", [P, 2, NB])
        vB = sb("vB", [P, 2, NB])
        tB = sb("tB", [P, 2, NB])
        rB = sb("rB", [P, 2, NB])
        rAB = sb("rAB", [P, 2, NB])
        vC = sb("vC", [P, 2, NB])
        rC = sb("rC", [P, 2, NB])
        x2 = two("x2", [P, D])
        ygT = sb("ygT", [P, 2, NG, JOINTS])
        hg = sb("hg", [P, HB2, NG, 2 * JOINTS])
        vgT = sb("vgT", [P, 2, NG, JOINTS])
        vg = sb("vg", [P, 2, D])
        og = sb("og", [P, 2, D])
        st2 = two("st2", [P, 6])
        mv2 = sb("mv2", [P, 2, 2])
        x3 = two("x3", [P, NB, D])
        xh = two("xh", [P, NB, D])
        xnT = two("xnT", [P, NODES])
        vs = two("vs", [P, NB, D])
        zT = two("zT", [P, NODES])
        tz = xh
        pre = two("pre", [P, NB, D])
        sp_abs = vs
        r3 = pre
        st3 = two("st3", [P, NB, 6])
        mv3 = two("mv3", [P, NB, 2])
        rs3 = two("rs3", [P, NB])
        yout = two("yout", [P, NB, D])

        bank = [ctx.enter_context(nc.psum_tensor(f"bank{i}", [P, 512], fp32)) for i in range(8)]

        def blocks(ap):
            return ap.rearrange("p (k n) -> p k n", k=NB)

        def flat4(tile):
            return tile[:, :, :, :].rearrange("p a s k -> p (a s k)")

        def wide(ap):
            return ap.rearrange("p k n -> p (k n)")

        weights_in = sem("weights_in")
        adj_in = [[sem(f"adj_in_{q}{s}") for s in range(2)] for q in range(2)]
        x_in = [[sem(f"x_in_{q}{s}") for s in range(2)] for q in range(2)]
        y_out = [sem(f"y_out_{s}") for s in range(2)]
        tr_ps = sem("tr_ps")
        agg_ps = sem("agg_ps")
        deg_ps = sem("deg_ps")
        bdT_ps = sem("bdT_ps")
        ahA_ps = sem("ahA_ps")
        hid_ps = sem("hid_ps")
        ssq_ps = sem("ssq_ps")
        rms_ps = sem("rms_ps")
        w2_ps = sem("w2_ps")
        o0_ps = sem("o0_ps")
        y_ps = sem("y_ps")
        o1_ps = sem("o1_ps")
        yg_ps = sem("yg_ps")
        hg_ps = sem("hg_ps")
        vgT_ps = sem("vgT_ps")
        vg_ps = sem("vg_ps")
        og_ps = sem("og_ps")
        fused_ps = sem("fused_ps")
        xhT_ps = sem("xhT_ps")
        v_ps = sem("v_ps")
        z_ps = sem("z_ps")
        zb_ps = sem("zb_ps")
        self_ps = sem("self_ps")
        adjT_sb = sem("adjT_sb")
        yT_sb = sem("yT_sb")
        aggT_sb = sem("aggT_sb")
        hid_sb = sem("hid_sb")
        sq_sb = sem("sq_sb")
        silu_sb = sem("silu_sb")
        outT_sb = sem("outT_sb")
        ygT_sb = sem("ygT_sb")
        vgT_sb = sem("vgT_sb")
        vg_sb = sem("vg_sb")
        xnT_sb = sem("xnT_sb")
        zT_sb = sem("zT_sb")
        act_abs = sem("act_abs")
        act_exp = sem("act_exp")
        act_ln = sem("act_ln")
        fus_exp = sem("fus_exp")
        setup_dve = sem("setup_dve")
        rowsum_sb = sem("rowsum_sb")
        r1_sb = sem("r1_sb")
        st1_sb = sem("st1_sb")
        mv1_sb = sem("mv1_sb")
        x2_sb = sem("x2_sb")
        deg_sb = sem("deg_sb")
        deg0_sb = sem("deg0_sb")
        sum0_sb = sem("sum0_sb")
        bd_sb = sem("bd_sb")
        ahT_sb = sem("ahT_sb")
        ahA_sb = sem("ahA_sb")
        ssq_sb = sem("ssq_sb")
        hgb_sb = sem("hgb_sb")
        hg_sb = sem("hg_sb")
        sq23_sb = sem("sq23_sb")
        sqsum = sem("sqsum")
        norm_sb = sem("norm_sb")
        ogb_sb = sem("ogb_sb")
        og_sb = sem("og_sb")
        r2_sb = sem("r2_sb")
        st2_sb = sem("st2_sb")
        mv2_sb = sem("mv2_sb")
        x3_sb = sem("x3_sb")
        xh_sb = sem("xh_sb")
        x3_rest_sb = sem("x3_rest_sb")
        xh_rest_sb = sem("xh_rest_sb")
        r0_sb = sem("r0_sb")
        st0_sb = sem("st0_sb")
        mv0_sb = sem("mv0_sb")
        x1_sb = sem("x1_sb")
        x1s_sb = sem("x1s_sb")
        vs_sb = sem("vs_sb")
        tz_sb = sem("tz_sb")
        pre_sb = sem("pre_sb")
        sp_sb = sem("sp_sb")
        r3_sb = sem("r3_sb")
        st3_sb = sem("st3_sb")
        mv3_sb = sem("mv3_sb")
        y_sb = sem("y_sb")
        half_sb = sem("half_sb")
        stat_sb = sem("stat_sb")
        rA_sb = sem("rA_sb")
        dinv_sb = sem("dinv_sb")
        rs0_sb = sem("rs0_sb")
        rs3_sb = sem("rs3_sb")
        ex_sb = sem("ex_sb")
        rms_sb = sem("rms_sb")
        sq01_sb = sem("sq01_sb")
        rC13_sb = sem("rC13_sb")
        rC0_sb = sem("rC0_sb")
        l1_step = sem("l1_step")
        rest_step = sem("rest_step")
        joint_step = sem("joint_step")
        deg_step = sem("deg_step")
        stat_step = sem("stat_step")
        l0_step = sem("l0_step")
        l3_step = sem("l3_step")
        x1b_sb = sem("x1b_sb")

        N_LOADS = 15 + 3 * NG
        SETUP = 9
        block = ctx.enter_context(nc.Block())

        def take_wait(n):
            nc.vector.memset(spare[:, n:n + 1], 0.0)

        def pairs_of(engine, body):
            body(0, 0, 0, True, False)
            body(1, 0, 1, True, True)
            with engine.Fori(0, (PAIRS - 2) // 2, 1) as i:
                body(2 * i + 2, i + 1, 0, True, True)
                body(2 * i + 3, i + 1, 1, True, True)
            body(PAIRS, PAIRS // 2, 0, False, True)

        def hidden_bank(s, k):
            return bank[(2, 3, 7)[(HB * s + k) % 3]]

        def ending(t):
            return isinstance(t, int) and t == PAIRS

        @block.sync
        def _(sp):
            loads = [(w1[:, :], l0_w1), (w2[:, :, :], l0_w2.rearrange("(k p) d -> p k d", p=P)),
                     (con[:, :], consts),
                     (wl1[:, :], l1_w), (wself[:, :], l3_self), (wneigh[:, :], l3_neigh),
                     (gw1[:, :, :], l2_w1.rearrange("g d h -> d g h")),
                     (bl1[:, :], l1_b.rearrange("(o d) -> o d", o=1).to_broadcast([P, D])),
                     (epsc[:, :], l0_eps.rearrange("(o d) -> o d", o=1).to_broadcast([P, 1])),
                     (fus[:, 0:NG], l2_fusion.rearrange("(o d) -> o d", o=1).to_broadcast([P, NG])),
                     (b2c[:, :], l0_b2.rearrange("(p o) -> p o", o=1)),
                     (gammac[:, :], l3_gamma.rearrange("(p o) -> p o", o=1)),
                     (betac[:, :], l3_beta.rearrange("(p o) -> p o", o=1)),
                     (b1c[:, :], l0_b1.rearrange("(k p) -> p k", p=P)),
                     (rmsc[:, :], l0_rms.rearrange("(k p) -> p k", p=P))]
            for g in range(NG):
                loads.append((gw2[:, g, :, :], l2_w2[g, :, :].rearrange("(k p) d -> p k d", p=P)))
                loads.append((gb1[:, :, g], l2_b1[g, :].rearrange("(k p) -> p k", p=P)))
                loads.append((gb2[g * JOINTS:(g + 1) * JOINTS, :], l2_b2[g:g + 1, :].to_broadcast([JOINTS, D])))
            assert len(loads) == N_LOADS

            def graph(tensor, g):
                if isinstance(g, int):
                    return tensor[g, :, :].rearrange("(k p) m -> p k m", p=P)
                return tensor[bass.ds(g, 1), :, :].rearrange("o (k p) m -> p (o k) m", p=P)

            def load(q, s, g):
                sp.dma_start(adjn[s][:, :, :], graph(adj, g)).then_inc(adj_in[q][s], 16)
                sp.dma_start(xin[q][s][:, :, :], graph(x, g)).then_inc(x_in[q][s], 16)

            load(0, 0, 0)
            for dst, src in loads[:3]:
                sp.dma_start(dst, src).then_inc(weights_in, 16)
            load(0, 1, 1)
            with nc.allow_non_contiguous_dma(reason="vectors of at most 512 values, once"):
                for dst, src in loads[3:]:
                    sp.dma_start(dst, src).then_inc(weights_in, 16)
            sp.wait_ge(ahA_sb, 1)
            for s in range(2):
                load(1, s, 2 + s)

            def store(g, pair, s):
                sp.wait_ge(y_sb, 4 * (2 * pair + s + 1))
                sp.dma_start(graph(out, g), yout[s][:, :, :]).then_inc(y_out[s], 16)

            def load_and_store(t, q):
                graphs = [sp.snap(2 * t + k) for k in (0, 1, -4, -3)]
                sp.wait_ge(ahA_sb, t)
                for s in range(2):
                    load(q, s, graphs[s])
                for s in range(2):
                    store(graphs[2 + s], t - 2, s)

            with sp.Fori(0, (PAIRS - 2) // 2, 1) as i:
                load_and_store(2 * i + 2, 0)
                load_and_store(2 * i + 3, 1)
            for pair in (PAIRS - 2, PAIRS - 1):
                for s in range(2):
                    store(2 * pair + s, pair, s)
            for s in range(2):
                sp.wait_ge(y_out[s], 16 * PAIRS)

        @block.tensor
        def _(pe):
            mm = nc.tensor.matmul
            tp = nc.tensor.transpose
            pe.wait_ge(weights_in, 16 * N_LOADS)
            pe.wait_ge(setup_dve, SETUP)

            def body(t, h, q, one, two_):
                u = t - 1
                three = not (isinstance(t, int) and t < 2)
                def a(s):
                    return 2 * t + s + 1

                def c(s):
                    return 2 * u + s + 1
                r = 1 - q

                def transpose_adjacency(s, j):
                    if s == 0 and j == 0:
                        pe.wait_ge(adj_in[q][0], 16 * h + 16)
                    if s == 1 and j == 0:
                        pe.wait_ge(adj_in[q][1], 16 * h + 16)
                    if s or j >= 2:
                        pe.wait_ge(adjT_sb, 4 * (2 * t + s) + j - 1)
                    elif two_ and j == 0:
                        pe.wait_ge(outT_sb, 2 * t - 1)
                    elif two_:
                        pe.wait_ge(r0_sb, 2 * t)
                    for i in range(NB):
                        last = tp(bank[j % 2][:, i * P:(i + 1) * P], adjn[s][:, i, j * P:(j + 1) * P], ident)
                    last.then_inc(tr_ps, 1)

                def neighbours1(s, j):
                    if j == 0:
                        pe.wait_ge(x1s_sb, c(s))
                        if s:
                            guard_prev(pe, pre_sb, t, 2)
                    last = mm(bank[3 - s][:, :], x1s[r][s][:, j, :], adjT[r][s][:, j, :],
                              start=(j == 0), stop=(j == NB - 1))
                    if j == NB - 1:
                        last.then_inc(y_ps, 1)

                def neighbours0(s, j):
                    if j == 0:
                        pe.wait_ge(adjT_sb, 4 * a(s))
                        pe.wait_ge(x_in[q][s], 16 * h + 16)
                        if s == 0 and two_:
                            pe.wait_ge(outT_sb, 2 * t)
                    mm(bank[4 if s == 0 else 0][:, :], xin[q][s][:, j, :], adjT[q][s][:, j, :],
                       start=(j == 0), stop=False)

                def self0(s):
                    pe.wait_ge(ex_sb, a(s))
                    b = bank[4 if s == 0 else 0]
                    for j in range(NB):
                        last = mm(b[:, j * P:(j + 1) * P], ex[s][:, j, :], ident, start=False,
                                  stop=(j == NB - 1), is_transpose=True)
                    last.then_inc(agg_ps, 1)

                def project1(s):
                    pe.wait_ge(yT_sb, c(s))
                    if s:
                        guard_prev(pe, tz_sb, t, 2)
                    b = bank[7 if s == 0 else 5]
                    for i in range(NB):
                        last = mm(b[:, i * P:(i + 1) * P], yT[s][:, i * P:(i + 1) * P], wl1[:, :],
                                  start=True, stop=True)
                    last.then_inc(o1_ps, 1)

                def hidden(s, k):
                    if k == 0:
                        pe.wait_ge(aggT_sb, a(s))
                    if HB * s + k >= 3:
                        pe.wait_ge(sq_sb, 8 * t + HB * s + k - 2)
                    elif HB * s + k == 2 and two_:
                        pe.wait_ge(r1_sb, c(0))
                    mm(hidden_bank(s, k)[:, :], w1[:, k * P:(k + 1) * P], aggT[s][:, :],
                       start=True, stop=True).then_inc(hid_ps, 1)

                def sum_squares(s):
                    pe.wait_ge(sqsum, a(s))
                    if s:
                        pe.wait_ge(ssq_sb, a(0))
                    for i in range(NB):
                        last = mm(bank[4][:, 2 * i:2 * i + 1], sqT[s][:, 0, i * P:(i + 1) * P], ones[:, :],
                                  start=True, stop=True)
                    last.then_inc(ssq_ps, 1)

                def spread_rms(s):
                    pe.wait_ge(rms_sb, a(s))
                    if s:
                        pe.wait_ge(norm_sb, 4 * a(0))
                    for i in range(NB):
                        last = tp(bank[1][:, i * P:(i + 1) * P], rms[s][:, i:i + 1].to_broadcast([P, P]), ident)
                    last.then_inc(rms_ps, 1)

                def project0(s, k):
                    if s == 0 and k == 0:
                        pe.wait_ge(ahA_sb, t + 1)
                    b = bank[0 if s == 0 else 4]
                    pe.wait_ge(silu_sb, 4 * a(s) - 4 + k + 1)
                    last = mm(b[:, :], w2[:, k, :], hT[s][:, k, :], start=(k == 0), stop=(k == HB - 1))
                    if k == HB - 1:
                        last.then_inc(w2_ps, 1)

                def rows0(s):
                    pe.wait_ge(outT_sb, a(s))
                    if s == 0:
                        pe.wait_ge(norm_sb, 4 * a(1))
                    else:
                        pe.wait_ge(r0_sb, a(0))
                    for i in range(NB):
                        last = tp(bank[1][:, i * P:(i + 1) * P], outT[s][:, i * P:(i + 1) * P], ident)
                    last.then_inc(o0_ps, 1)

                for j in range(NB):
                    if two_:
                        neighbours1(0, j)
                for j in range(NB):
                    if one:
                        transpose_adjacency(0, j)
                    if two_:
                        neighbours1(1, j)
                if two_:
                    guard_prev(pe, pre_sb, t, 1)
                    project1(0)
                for j in range(NB):
                    if one:
                        transpose_adjacency(1, j)
                        neighbours0(0, j)
                    if two_ and j == 1:
                        project1(1)
                if one:
                    self0(0)
                    for j in range(NB):
                        neighbours0(1, j)
                    self0(1)
                    for s in range(2):
                        o = bank[1][0:GI, 32 * s:32 * s + JOINTS]
                        mm(o, const("spread"), adjn[s][:, 0, 0:JOINTS], start=True, stop=False)
                        last = mm(o, const("spread"), ident[:, 0:JOINTS], start=False, stop=True)
                    last.then_inc(deg_ps, 1)
                    for k in range(HB):
                        hidden(0, k)
                if two_:
                    pe.wait_ge(x2_sb, c(1))
                    for s in range(2):
                        last = mm(bank[6][:, s * GI:(s + 1) * GI], x2[s][:, :], ahatA[r][s][:, :],
                                  start=True, stop=True)
                    last.then_inc(yg_ps, 1)
                if one:
                    hidden(1, 0)
                    hidden(1, 1)
                    hidden(1, 2)
                    sum_squares(0)
                if two_:
                    pe.wait_ge(ygT_sb, u + 1)
                    for k in range(HB2):
                        for g in range(NG):
                            at = (k * NG + g) * 2 * JOINTS
                            last = mm(bank[5][:, at:at + 2 * JOINTS], gw1[:, g, k * P:(k + 1) * P],
                                      ygT[:, :, g, :], start=True, stop=True)
                    last.then_inc(hg_ps, 1)
                if one:
                    pe.wait_ge(bd_sb, t + 1)
                    pe.wait_ge(aggT_sb, a(1))
                    for g in range(2):
                        last = tp(bank[0][0:GI, P * g:P * g + GI], bd[g][0:GI, :], ident[0:GI, 0:GI])
                    last.then_inc(bdT_ps, 1)
                    hidden(1, 3)
                    spread_rms(0)
                if two_:
                    pe.wait_ge(hg_sb, u + 1)
                    for g in range(NG):
                        at = g * 2 * JOINTS
                        for k in range(HB2):
                            last = mm(bank[6][:, at:at + 2 * JOINTS], gw2[:, g, k, :], hg[:, k, g, :],
                                      start=(k == 0), stop=(k == HB2 - 1))
                    last.then_inc(vgT_ps, 1)
                if one:
                    pe.wait_ge(ahT_sb, t + 1)
                    for g in range(2):
                        last = mm(bank[0][:, P * g:P * g + GI], const("gather", GI), ahatT[q][g][0:GI, :],
                                  start=True, stop=True)
                    last.then_inc(ahA_ps, 1)
                if two_:
                    pe.wait_ge(vgT_sb, u + 1)
                    for s in range(2):
                        last = tp(bank[5][0:GI, s * D:(s + 1) * D], vgT[:, s, :, :].rearrange("p g i -> p (g i)"), ident)
                    last.then_inc(vg_ps, 1)
                if one:
                    project0(0, 0)
                    sum_squares(1)
                    project0(0, 1)
                if two_:
                    pe.wait_ge(vg_sb, u + 1)
                    for s in range(2):
                        last = mm(bank[6][0:GI, s * D:(s + 1) * D], ahatT[r][s][0:GI, :], vg[0:GI, s, :],
                                  start=True, stop=True)
                    last.then_inc(og_ps, 1)
                if one:
                    spread_rms(1)
                    project0(0, 2)
                    project0(0, 3)
                if two_:
                    pe.wait_ge(og_sb, u + 1)
                    mm(bank[5][:, 0:2 * D], selw[0:GI, :], wide(og[0:GI, :, :]), start=True, stop=True).then_inc(fused_ps, 1)
                if one:
                    project0(1, 0)
                    project0(1, 1)
                    project0(1, 2)
                    rows0(0)
                    project0(1, 3)
                if two_:
                    for s in range(2):
                        pe.wait_ge(xh_rest_sb, c(s))
                        if s == 0:
                            pe.wait_ge(ogb_sb, u + 1)
                        elif one:
                            pe.wait_ge(sq_sb, 8 * t + 8)
                        for i in range(1, NB):
                            tp(bank[6 + s][:, i * P:(i + 1) * P], xh[s][:, i, :], ident)
                    if one:
                        rows0(1)
                    for s in range(2):
                        pe.wait_ge(xh_sb, c(s))
                        tp(bank[6 + s][:, 0:P], xh[s][:, 0, :], ident).then_inc(xhT_ps, 1)
                    for s in range(2):
                        pe.wait_ge(xnT_sb, c(s))
                        if s == 0:
                            pe.wait_ge(r2_sb, c(1))
                        for i in range(NB):
                            last = mm(bank[5 + s][:, i * P:(i + 1) * P], xnT[s][:, i * P:(i + 1) * P],
                                      wneigh[:, :], start=True, stop=True)
                        last.then_inc(v_ps, 1)
                    for s in range(2):
                        pe.wait_ge(vs_sb, c(s))
                        if s == 0:
                            pe.wait_ge(xnT_sb, c(1))
                        b = bank[7 if s == 0 else 5]
                        for j in range(NB):
                            last = mm(b[:, :], vs[s][:, j, :], adjT[r][s][:, j, :], start=(j == 0), stop=(j == NB - 1))
                        last.then_inc(z_ps, 1)
                    for s in range(2):
                        pe.wait_ge(zT_sb, c(s))
                        if s == 0:
                            pe.wait_ge(vs_sb, c(1))
                        b = bank[6 if s == 0 else 5]
                        for i in range(NB):
                            last = tp(b[:, i * P:(i + 1) * P], zT[s][:, i * P:(i + 1) * P], ident)
                        last.then_inc(zb_ps, 1)
                        b = bank[7 if s == 0 else 2]
                        for i in range(NB):
                            last = mm(b[:, i * P:(i + 1) * P], xnT[s][:, i * P:(i + 1) * P], wsum[:, :],
                                      start=True, stop=True)
                        last.then_inc(self_ps, 1)
                elif one:
                    rows0(1)

            def guard_prev(eng, what, t, k):
                if isinstance(t, int) and t == 1:
                    return
                eng.wait_ge(what, 2 * t - 4 + k)

            pairs_of(pe, body)

        @block.scalar
        def _(act):
            A = nc.scalar.activation
            act.wait_ge(weights_in, 16 * N_LOADS)
            act.wait_ge(setup_dve, 2)
            A(fus[:, 15:20], fus[:, 10:15], ACT.Exp).then_inc(fus_exp, 1)

            def body(t, h, q, one, two_):
                u = t - 1
                three = not (isinstance(t, int) and t < 2)

                def a(s):
                    return 2 * t + s + 1

                def c(s):
                    return 2 * u + s + 1

                def adjacency(s):
                    for j in range(NB):
                        act.wait_ge(tr_ps, 4 * (2 * t + s) + j + 1)
                        A(adjT[q][s][:, j, :], bank[j % 2][:, :], ACT.Identity,
                          accum_out=sums[q][:, 1, s, j:j + 1]).then_inc(adjT_sb, 1)

                def neighbours1(s):
                    act.wait_ge(y_ps, c(s))
                    A(yT[s][:, :], bank[3 - s][:, :], ACT.Identity).then_inc(yT_sb, 1)

                def neighbours0(s):
                    act.wait_ge(agg_ps, a(s))
                    A(aggT[s][:, :], bank[4 if s == 0 else 0][:, :], ACT.Identity).then_inc(aggT_sb, 1)

                def softplus_exp(p):
                    for s in range(2):
                        act.wait_ge(pre_sb, 2 * p + s + 1)
                        A(wide(sp_abs[s][:, :, :]), wide(pre[s][:, :, :]), ACT.Abs).then_inc(act_abs, 1)
                    for s in range(2):
                        act.wait_ge(act_abs, 2 * p + s + 1)
                        e = wide(sp_abs[s][:, :, :])
                        A(e, e, ACT.Exp, scale=-1.0).then_inc(act_exp, 1)

                def softplus_ln(p):
                    for s in range(2):
                        act.wait_ge(act_exp, 2 * p + s + 1)
                        e = wide(sp_abs[s][:, :, :])
                        A(e, e, ACT.Ln, bias=1.0).then_inc(act_ln, 1)

                def hidden(s):
                    for k in range(HB):
                        act.wait_ge(hid_ps, 4 * (2 * t + s) + k + 1)
                        A(hT[s][:, k, :], hidden_bank(s, k)[:, :], ACT.Identity, bias=b1c[:, k:k + 1]).then_inc(hid_sb, 1)
                        A(sqT[s][:, k, :], hidden_bank(s, k)[:, :], ACT.Square, bias=b1c[:, k:k + 1]).then_inc(sq_sb, 1)

                if three:
                    softplus_exp(t - 2)
                if two_:
                    neighbours1(0)
                if one:
                    adjacency(0)
                if two_:
                    neighbours1(1)
                if one:
                    adjacency(1)
                    neighbours0(0)
                if three:
                    softplus_ln(t - 2)
                if one:
                    neighbours0(1)
                    hidden(0)
                if two_:
                    act.wait_ge(yg_ps, u + 1)
                    A(ygT[:, :, :, :].rearrange("p s g i -> p (s g i)"), bank[6][:, 0:2 * GI], ACT.Identity).then_inc(ygT_sb, 1)
                if one:
                    hidden(1)

                def silu(s):
                    for k in range(HB):
                        act.wait_ge(norm_sb, 4 * (2 * t + s) + k + 1)
                        A(hT[s][:, k, :], hT[s][:, k, :], ACT.Silu, scale=rmsc[:, k:k + 1]).then_inc(silu_sb, 1)

                def l0_out(s):
                    act.wait_ge(w2_ps, a(s))
                    A(outT[s][:, :], bank[0 if s == 0 else 4][:, :], ACT.Identity, bias=b2c[:, 0:1]).then_inc(outT_sb, 1)

                if one:
                    silu(0)
                    silu(1)
                    l0_out(0)
                    l0_out(1)
                if two_:
                    for s in range(2):
                        act.wait_ge(xhT_ps, c(s))
                        A(xnT[s][:, :], bank[6 + s][:, :], ACT.Identity, bias=betac[:, 0:1],
                          scale=gammac[:, 0:1]).then_inc(xnT_sb, 1)
                    for s in range(2):
                        act.wait_ge(z_ps, c(s))
                        A(zT[s][:, :], bank[7 if s == 0 else 5][:, :], ACT.Identity).then_inc(zT_sb, 1)
                if ending(t):
                    softplus_exp(t - 1)
                    softplus_ln(t - 1)

            pairs_of(act, body)

        @block.vector
        def _(dve):
            V = nc.vector

            dve.wait_ge(weights_in, 16 * N_LOADS)
            V.reduce_max(fus[:, 5:6], fus[:, 0:NG], AX.X).then_inc(setup_dve, 1)
            dve.wait_ge(setup_dve, 1)
            V.tensor_scalar(fus[:, 10:15], fus[:, 0:NG], fus[:, 5:6], None, ALU.subtract).then_inc(setup_dve, 1)
            V.tensor_tensor(wsum[:, :], wself[:, :], wneigh[:, :], ALU.add).then_inc(setup_dve, 1)
            V.memset(ones[:, :], 1.0).then_inc(setup_dve, 1)
            dve.wait_ge(fus_exp, 1)
            V.tensor_reduce(fus[:, 6:7], fus[:, 15:20], AX.X, ALU.add).then_inc(setup_dve, 1)
            V.tensor_tensor(fus[:, 20:25], fus[:, 15:20], const("group"), ALU.mult).then_inc(setup_dve, 1)
            dve.wait_ge(setup_dve, 6)
            V.reciprocal(fus[:, 7:8], fus[:, 6:7]).then_inc(setup_dve, 1)
            V.tensor_reduce(fus[:, 8:9], fus[:, 20:25], AX.X, ALU.add).then_inc(setup_dve, 1)
            dve.wait_ge(setup_dve, 8)
            V.tensor_scalar(selw[:, :], const("select"), fus[:, 7:8], fus[:, 8:9], ALU.mult, ALU.mult).then_inc(setup_dve, 1)

            def body(t, h, q, one, two_):
                u = t - 1
                three = not (isinstance(t, int) and t < 2)
                r = 1 - q

                def a(s):
                    return 2 * t + s + 1

                def c(s):
                    return 2 * u + s + 1

                if one:
                    for s in range(2):
                        dve.wait_ge(adj_in[q][s], 16 * h + 16)
                        V.tensor_reduce(sums[q][:, 0, s, :], adjn[s][:, :, :], AX.X, ALU.add).then_inc(rowsum_sb, 1)
                if two_:
                    for s in range(2):
                        dve.wait_ge(o1_ps, c(s))
                        dve.wait_ge(x1b_sb, c(s))
                        for i in range(NB):
                            last = V.scalar_tensor_tensor(
                                out=r1[s][:, i, :], in0=bank[7 if s == 0 else 5][:, i * P:(i + 1) * P],
                                scalar=scal[r][:, 0, s, i:i + 1], in1=x1b[r][s][:, i, :], op0=ALU.mult, op1=ALU.add)
                        last.then_inc(r1_sb, 1)
                    for s in range(2):
                        dve.wait_ge(r1_sb, c(s))
                        for i in range(NB):
                            last = V.bn_stats(st1[s][:, i, :], r1[s][:, i, :])
                        last.then_inc(st1_sb, 1)
                    for s in range(2):
                        dve.wait_ge(st1_sb, c(s))
                        take_wait(s)
                        for i in range(NB):
                            last = V.bn_aggr(mv1[:, s, i, :], st1[s][:, i, :])
                        last.then_inc(mv1_sb, 1)
                def softplus_stats(p, s):
                    n = 2 * p + s + 1
                    dve.wait_ge(act_ln, n)
                    V.scalar_tensor_tensor(out=pre[s][:, :, :], in0=pre[s][:, :, :], scalar=0.0,
                                           in1=sp_abs[s][:, :, :], op0=ALU.max, op1=ALU.add).then_inc(sp_sb, 1)
                    dve.wait_ge(sp_sb, n)
                    V.tensor_tensor(r3[s][:, :, :], pre[s][:, :, :], x3[s][:, :, :], ALU.add).then_inc(r3_sb, 1)
                    dve.wait_ge(r3_sb, n)
                    for i in range(NB):
                        last = V.bn_stats(st3[s][:, i, :], r3[s][:, i, :])
                    last.then_inc(st3_sb, 1)
                    dve.wait_ge(st3_sb, n)
                    take_wait(6 + s)
                    for i in range(NB):
                        last = V.bn_aggr(mv3[s][:, i, :], st3[s][:, i, :])
                    last.then_inc(mv3_sb, 1)

                def result(p, s):
                    dve.wait_ge(rs3_sb, 2 * p + s + 1)
                    if not (isinstance(p, int) and p == 0):
                        dve.wait_ge(y_out[s], 16 * p)
                    for i in range(NB):
                        V.tensor_scalar(yout[s][:, i, :], r3[s][:, i, :], mv3[s][:, i, 0:1], rs3[s][:, i:i + 1],
                                        ALU.subtract, ALU.mult).then_inc(y_sb, 1)

                def mean_square(s):
                    dve.wait_ge(ssq_ps, a(s))
                    V.tensor_scalar(ssq[s][:, :], bank[4][:, 0:2 * NB].rearrange("p (k o) -> p k o", o=2)[:, :, 0],
                                    1.0 / HID, RMS_EPS, ALU.mult, ALU.add).then_inc(ssq_sb, 1)

                def add_squares(s):
                    dve.wait_ge(sq_sb, 4 * a(s))
                    V.tensor_tensor(sqT[s][:, 2, :], sqT[s][:, 2, :], sqT[s][:, 3, :], ALU.add).then_inc(sq23_sb, 1)
                    dve.wait_ge(sq23_sb, a(s))
                    dve.wait_ge(sq01_sb, a(s))
                    V.tensor_tensor(sqT[s][:, 0, :], sqT[s][:, 0, :], sqT[s][:, 2, :], ALU.add).then_inc(sqsum, 1)

                def normalise(s, k):
                    if k == 0:
                        dve.wait_ge(rms_ps, a(s))
                        dve.wait_ge(hid_sb, 4 * a(s))
                    V.tensor_tensor(hT[s][:, k, :], hT[s][:, k, :], bank[1][:, :], ALU.mult).then_inc(norm_sb, 1)

                def l2_norm(s, lo, hi, x3_done, xh_done):
                    for i in range(lo, hi):
                        last = V.tensor_scalar(x3[s][:, i, :], r1[s][:, i, :], mv1[:, s, i, 0:1], rAB[:, s, i:i + 1],
                                               ALU.subtract, ALU.mult)
                    last.then_inc(x3_done, 1)
                    dve.wait_ge(x3_done, c(s))
                    V.tensor_tensor(xh[s][:, lo:hi, :], x3[s][:, lo:hi, :],
                                    rC[:, s, lo:hi].rearrange("p (k o) -> p k o", o=1).to_broadcast([P, hi - lo, D]),
                                    ALU.mult).then_inc(xh_done, 1)

                if three:
                    softplus_stats(t - 2, 0)
                if one:
                    dve.wait_ge(deg_ps, t + 1)
                    for s in range(2):
                        V.tensor_tensor_reduce(out=degj[s][0:GI, :], in0=bank[1][0:GI, 32 * s:32 * s + JOINTS],
                                               in1=const("member", GI), scale=1.0, scalar=0.0, op0=ALU.mult,
                                               op1=ALU.add, accum_out=deg[0:GI, s:s + 1]).then_inc(deg_sb, 1)
                    dve.wait_ge(deg_sb, 2 * t + 2)
                    V.tensor_scalar(degz[0:GI, 0:2], deg[0:GI, :], 0.0, None, ALU.is_equal).then_inc(deg0_sb, 1)
                    dve.wait_ge(rowsum_sb, 2 * t + 2)
                    dve.wait_ge(adjT_sb, 8 * t + 8)
                    V.tensor_scalar(flat4(zer), flat4(sums[q]), 0.0, None, ALU.is_equal).then_inc(sum0_sb, 1)
                if two_:
                    for s in range(2):
                        dve.wait_ge(rA_sb, u + 1)
                        dve.wait_ge(mv1_sb, c(s))
                        V.tensor_scalar(x2[s][:, :], r1[s][:, 0, :], mv1[:, s, 0, 0:1], rA[:, s, 0:1],
                                        ALU.subtract, ALU.mult).then_inc(x2_sb, 1)
                if three:
                    softplus_stats(t - 2, 1)
                if one:
                    dve.wait_ge(dinv_sb, t + 1)
                    for s in range(2):
                        last = V.scalar_tensor_tensor(
                            out=bd[s][0:GI, :].rearrange("p (g j) -> p g j", g=NG),
                            in0=bank[1][0:GI, 32 * s:32 * s + JOINTS].rearrange("p (o j) -> p o j", o=1)
                            .to_broadcast([GI, NG, JOINTS]),
                            scalar=dinv[0:GI, s:s + 1],
                            in1=const("block", GI).rearrange("p (g j) -> p g j", g=NG), op0=ALU.mult, op1=ALU.mult)
                    last.then_inc(bd_sb, 1)
                    add_squares(0)
                if three:
                    result(t - 2, 0)
                if one:
                    mean_square(0)
                if three:
                    result(t - 2, 1)
                if two_:
                    dve.wait_ge(hg_ps, u + 1)
                    n = HB2 * NG
                    hflat = hg[:, :, :, :].rearrange("p k g i -> p (k g) i")
                    V.tensor_tensor(hflat, bank[5][:, 0:n * 2 * JOINTS].rearrange("p (n i) -> p n i", n=n),
                                    gb1[:, :, :].rearrange("p k (g o) -> p (k g) o", o=1).to_broadcast([P, n, 2 * JOINTS]),
                                    ALU.add).then_inc(hgb_sb, 1)
                    dve.wait_ge(hgb_sb, u + 1)
                    V.tensor_scalar(hflat, hflat, 0.0, None, ALU.max).then_inc(hg_sb, 1)
                if one:
                    dve.wait_ge(bdT_ps, t + 1)
                    for s in range(2):
                        last = V.tensor_scalar(ahatT[q][s][0:GI, :], bank[0][0:GI, P * s:P * s + GI],
                                               dinv[0:GI, s:s + 1], None, ALU.mult)
                    last.then_inc(ahT_sb, 1)
                    for k in range(HB):
                        normalise(0, k)
                if two_:
                    dve.wait_ge(vgT_ps, u + 1)
                    V.tensor_copy(vgT[:, :, :, :].rearrange("p s g i -> p g s i"),
                                  bank[6][:, 0:2 * GI].rearrange("p (g s i) -> p g s i", g=NG, s=2)).then_inc(vgT_sb, 1)
                if one:
                    add_squares(1)
                    dve.wait_ge(ahA_ps, t + 1)
                    for s in range(2):
                        last = V.tensor_copy(ahatA[q][s][:, :], bank[0][:, P * s:P * s + GI])
                    last.then_inc(ahA_sb, 1)
                if two_:
                    dve.wait_ge(vg_ps, u + 1)
                    V.tensor_copy(wide(vg[0:GI, :, :]), bank[5][0:GI, 0:2 * D]).then_inc(vg_sb, 1)
                if one:
                    mean_square(1)
                if two_:
                    dve.wait_ge(rC13_sb, u + 1)
                    for s in range(2):
                        l2_norm(s, 1, NB, x3_rest_sb, xh_rest_sb)
                if two_:
                    dve.wait_ge(og_ps, u + 1)
                    V.tensor_tensor(og[0:GI, :, :], bank[6][0:GI, 0:2 * D].rearrange("p (s d) -> p s d", s=2),
                                    gb2[0:GI, :].rearrange("p (o d) -> p o d", o=1).to_broadcast([GI, 2, D]),
                                    ALU.add).then_inc(ogb_sb, 1)
                    dve.wait_ge(ogb_sb, u + 1)
                    V.tensor_scalar(og[0:GI, :, :], og[0:GI, :, :], 0.0, None, ALU.max).then_inc(og_sb, 1)
                if one:
                    for k in range(HB):
                        normalise(1, k)
                if two_:
                    dve.wait_ge(fused_ps, u + 1)
                    for s in range(2):
                        V.tensor_tensor(r1[s][:, 0, :], bank[5][:, s * D:(s + 1) * D], x2[s][:, :],
                                        ALU.add).then_inc(r2_sb, 1)
                    for s in range(2):
                        dve.wait_ge(r2_sb, c(s))
                        V.bn_stats(st2[s][:, :], r1[s][:, 0, :]).then_inc(st2_sb, 1)
                    dve.wait_ge(l1_step, 3 * u + 2)
                    for s in range(2):
                        dve.wait_ge(st2_sb, c(s))
                        take_wait(2 + s)
                        V.bn_aggr(mv1[:, s, 0, :], st2[s][:, :]).then_inc(mv2_sb, 1)

                def l0_residual(s):
                    dve.wait_ge(o0_ps, a(s))
                    V.tensor_tensor(wide(r0[s][:, :, :]), bank[1][:, :], wide(xin[q][s][:, :, :]), ALU.add).then_inc(r0_sb, 1)
                    dve.wait_ge(r0_sb, a(s))
                    for i in range(NB):
                        last = V.bn_stats(st0[s][:, i, :], r0[s][:, i, :])
                    last.then_inc(st0_sb, 1)
                    dve.wait_ge(st0_sb, a(s))
                    take_wait(4 + s)
                    for i in range(NB):
                        last = V.bn_aggr(mv0[s][:, i, :], st0[s][:, i, :])
                    last.then_inc(mv0_sb, 1)

                def l0_norm(s):
                    dve.wait_ge(rs0_sb, a(s))
                    for i in range(NB):
                        last = V.tensor_scalar(x1[s][:, i, :], r0[s][:, i, :], mv0[s][:, i, 0:1], rs0[s][:, i:i + 1],
                                               ALU.subtract, ALU.mult)
                    last.then_inc(x1_sb, 1)
                    dve.wait_ge(x1_sb, a(s))
                    dve.wait_ge(stat_sb, t + 1)
                    V.tensor_tensor(x1s[q][s][:, :, :], x1[s][:, :, :],
                                    scal[q][:, 0, s, :].rearrange("p (k o) -> p k o", o=1).to_broadcast([P, NB, D]),
                                    ALU.mult).then_inc(x1s_sb, 1)

                def l3_values(s):
                    dve.wait_ge(v_ps, c(s))
                    V.tensor_tensor(vs[s][:, :, :], blocks(bank[5 + s][:, :]),
                                    scal[r][:, 1, s, :].rearrange("p (k o) -> p k o", o=1).to_broadcast([P, NB, D]),
                                    ALU.mult).then_inc(vs_sb, 1)

                if one:
                    l0_residual(0)
                if two_:
                    dve.wait_ge(rC0_sb, u + 1)
                    for s in range(2):
                        l2_norm(s, 0, 1, x3_sb, xh_sb)
                if one:
                    l0_residual(1)
                if two_:
                    l3_values(0)
                    l3_values(1)
                if one:
                    l0_norm(0)
                    l0_norm(1)
                if two_:
                    for s in range(2):
                        dve.wait_ge(zb_ps, c(s))
                        V.tensor_tensor(tz[s][:, :, :], blocks(bank[6 if s == 0 else 5][:, :]),
                                        scal[r][:, 2, s, :].rearrange("p (k o) -> p k o", o=1).to_broadcast([P, NB, D]),
                                        ALU.mult).then_inc(tz_sb, 1)
                        dve.wait_ge(self_ps, c(s))
                        dve.wait_ge(tz_sb, c(s))
                        V.tensor_tensor(pre[s][:, :, :], blocks(bank[7 if s == 0 else 2][:, :]), tz[s][:, :, :],
                                        ALU.add).then_inc(pre_sb, 1)
                if ending(t):
                    for s in range(2):
                        softplus_stats(t - 1, s)
                    for s in range(2):
                        result(t - 1, s)

            pairs_of(dve, body)

        @block.gpsimd
        def _(pool):
            G = nc.gpsimd
            for tile, value in ((half, -0.5), (ln_eps, LN_EPS), (deg_eps, DEG_EPS), (zeros, 0.0), (unit, 1.0)):
                G.memset(tile[:, :], value).then_inc(half_sb, 1)
            pool.wait_ge(weights_in, 16 * N_LOADS)
            pool.wait_ge(half_sb, 5)

            def slots(tile):
                return tile[:, 0:2 * NB].rearrange("p (s k) -> p s k", s=2)

            def rsqrt(out_, in_, n, what):
                G.tensor_tensor(out_, in_, half[0:in_.shape[0], 0:n], ALU.pow).then_inc(what, 1)

            def body(t, h, q, one, two_):
                u = t - 1
                three = not (isinstance(t, int) and t < 2)

                def a(s):
                    return 2 * t + s + 1

                def c(s):
                    return 2 * u + s + 1

                def last_scale(p, s):
                    n = 2 * p + s + 1
                    pool.wait_ge(mv3_sb, n)
                    G.tensor_tensor(mv3[s][:, :, 1], mv3[s][:, :, 1], ln_eps[:, 0:NB], ALU.add).then_inc(l3_step, 1)
                    pool.wait_ge(l3_step, n)
                    rsqrt(rs3[s][:, :], mv3[s][:, :, 1], NB, rs3_sb)

                if one:
                    for s in range(2):
                        pool.wait_ge(x_in[q][s], 16 * h + 16)
                        if two_:
                            pool.wait_ge(agg_ps, 2 * t - 1 + s)
                        G.tensor_tensor(wide(ex[s][:, :, :]), wide(xin[q][s][:, :, :]),
                                        epsc[:, 0:1].to_broadcast([P, NB * D]), ALU.mult).then_inc(ex_sb, 1)
                if two_:
                    pool.wait_ge(mv1_sb, c(1))
                    if not (isinstance(t, int) and t == 1):
                        pool.wait_ge(xh_sb, c(1) - 2)
                    v = mv1[:, :, :, 1]
                    G.tensor_tensor(vE[:, :, :], v, slots(ln_eps), ALU.add).then_inc(l1_step, 1)
                    pool.wait_ge(l1_step, 3 * u + 1)
                    rsqrt(wide(rA[:, :, :]), wide(vE[:, :, :]), 2 * NB, rA_sb)
                    pool.wait_ge(rA_sb, u + 1)
                    G.tensor_tensor(tB[:, :, :], v, rA[:, :, :], ALU.mult).then_inc(l1_step, 1)
                    pool.wait_ge(l1_step, 3 * u + 2)
                    G.tensor_tensor(vB[:, :, :], tB[:, :, :], rA[:, :, :], ALU.mult).then_inc(l1_step, 1)
                if one:
                    pool.wait_ge(deg0_sb, t + 1)
                    d = degz[0:GI, :]
                    G.tensor_tensor(d[:, 2:4], deg[0:GI, :], d[:, 0:2], ALU.add).then_inc(deg_step, 1)
                    pool.wait_ge(deg_step, 4 * t + 1)
                    rsqrt(d[:, 4:6], d[:, 2:4], 2, deg_step)
                    G.tensor_tensor(d[:, 0:2], unit[0:GI, 0:2], d[:, 0:2], ALU.subtract).then_inc(deg_step, 1)
                    pool.wait_ge(deg_step, 4 * t + 3)
                    G.tensor_tensor(d[:, 0:2], d[:, 0:2], d[:, 4:6], ALU.mult).then_inc(deg_step, 1)
                    pool.wait_ge(deg_step, 4 * t + 4)
                    G.tensor_tensor(dinv[0:GI, :], d[:, 0:2], const("own", GI).to_broadcast([GI, 2]), ALU.mult).then_inc(dinv_sb, 1)

                def add_squares(s):
                    pool.wait_ge(sq_sb, 4 * (2 * t + s) + 2)
                    G.tensor_tensor(sqT[s][:, 0, :], sqT[s][:, 0, :], sqT[s][:, 1, :], ALU.add).then_inc(sq01_sb, 1)

                def inverse_rms(s):
                    pool.wait_ge(ssq_sb, a(s))
                    rsqrt(rms[s][:, :], ssq[s][:, :], NB, rms_sb)

                def later_scales(lo, hi, var, step, at, done):
                    n = hi - lo
                    b = (slice(None), slice(None), slice(lo, hi))
                    eps = slots(ln_eps)[:, :, 0:n]
                    power = half[:, 0:2 * NB].rearrange("p (s k) -> p s k", s=2)[:, :, 0:n]
                    G.tensor_tensor(tB[b], var, eps, ALU.add).then_inc(step, 1)
                    pool.wait_ge(step, at + 1)
                    G.tensor_tensor(rB[b], tB[b], power, ALU.pow).then_inc(step, 1)
                    pool.wait_ge(step, at + 2)
                    G.tensor_tensor(vC[b], var, rB[b], ALU.mult).then_inc(step, 1)
                    pool.wait_ge(step, at + 3)
                    G.tensor_tensor(vC[b], vC[b], rB[b], ALU.mult).then_inc(step, 1)
                    pool.wait_ge(step, at + 4)
                    G.tensor_tensor(vC[b], vC[b], eps, ALU.add).then_inc(step, 1)
                    first = lo == 0
                    G.tensor_tensor(rAB[b], slots(unit)[:, :, 0:n] if first else rA[b], rB[b], ALU.mult).then_inc(step, 1)
                    pool.wait_ge(step, at + 6)
                    G.tensor_tensor(rC[b], vC[b], power, ALU.pow).then_inc(done, 1)

                if one:
                    add_squares(0)
                if three:
                    last_scale(t - 2, 0)
                    last_scale(t - 2, 1)
                if one:
                    inverse_rms(0)
                    add_squares(1)
                if two_:
                    pool.wait_ge(l1_step, 3 * u + 3)
                    later_scales(1, NB, vB[:, :, 1:NB], rest_step, 6 * u, rC13_sb)
                if one:
                    inverse_rms(1)
                    pool.wait_ge(sum0_sb, t + 1)
                    if two_ and not (isinstance(t, int) and t == 1):
                        pool.wait_ge(tz_sb, 2 * t - 2)
                    S = sums[q]
                    G.tensor_tensor(pw[:, 0, :, :], S[:, 0, :, :], slots(deg_eps), ALU.add).then_inc(stat_step, 1)
                    G.tensor_tensor(pw[:, 1:3, :, :], S[:, :, :, :], zer[:, :, :, :], ALU.add).then_inc(stat_step, 1)
                    pool.wait_ge(stat_step, 5 * t + 2)
                    G.tensor_tensor(zr[:, 0, :, :], slots(unit), zer[:, 0, :, :], ALU.subtract).then_inc(stat_step, 1)
                    G.tensor_tensor(zr[:, 1, :, :], zer[:, 1, :, :], slots(unit), ALU.subtract).then_inc(stat_step, 1)
                    flat = scal[q][:, :, :, :].rearrange("p a s k -> p (a s k)")
                    rsqrt(flat, pw[:, :, :, :].rearrange("p a s k -> p (a s k)"), 24, stat_step)
                    pool.wait_ge(stat_step, 5 * t + 5)
                    G.tensor_tensor(scal[q][:, 1:3, :, :], scal[q][:, 1:3, :, :], zr[:, :, :, :], ALU.mult).then_inc(stat_sb, 1)
                if two_:
                    pool.wait_ge(mv2_sb, c(1))
                    later_scales(0, 1, mv1[:, :, 0:1, 1], joint_step, 6 * u, rC0_sb)

                def l0_scale(s):
                    pool.wait_ge(mv0_sb, a(s))
                    G.tensor_tensor(mv0[s][:, :, 1], mv0[s][:, :, 1], ln_eps[:, 0:NB], ALU.add).then_inc(l0_step, 1)
                    pool.wait_ge(l0_step, a(s))
                    rsqrt(rs0[s][:, :], mv0[s][:, :, 1], NB, rs0_sb)

                def l0_bias(s):
                    pool.wait_ge(x1_sb, a(s))
                    G.tensor_tensor(x1b[q][s][:, :, :], x1[s][:, :, :],
                                    bl1[:, :].rearrange("p (o d) -> p o d", o=1).to_broadcast([P, NB, D]),
                                    ALU.add).then_inc(x1b_sb, 1)

                if one:
                    l0_scale(0)
                    l0_scale(1)
                    l0_bias(0)
                    l0_bias(1)
                if ending(t):
                    last_scale(t - 1, 0)
                    last_scale(t - 1, 1)

            pairs_of(pool, body)


INPUTS = ['x', 'adj', 'L0_gnn_epsilon', 'L0_gnn_W1', 'L0_gnn_b1', 'L0_gnn_rms_weight', 'L0_gnn_W2', 'L0_gnn_b2',
          'L1_gnn_weight', 'L1_gnn_bias', 'L2_gnn_W1', 'L2_gnn_b1', 'L2_gnn_W2', 'L2_gnn_b2', 'L2_gnn_fusion_w',
          'L3_gnn_gamma', 'L3_gnn_beta', 'L3_gnn_W_self', 'L3_gnn_W_neigh']


def kernel(**inputs):
    import concourse.bacc as bacc
    from concourse.bass_utils import run_bass_kernel_spmd

    nc = bacc.Bacc("TRN2", target_bir_lowering=False, num_devices=1)
    arrays, args = {}, []
    for name in INPUTS:
        a = np.ascontiguousarray(np.asarray(inputs[name]))
        if a.ndim == 0 or name == 'L0_gnn_epsilon':
            a = a.reshape(1)
        arrays[name] = a
    arrays["shape_constants"] = shape_constants()
    for name, a in arrays.items():
        args.append(nc.dram_tensor(name, a.shape, mybir.dt.from_np(a.dtype), kind="ExternalInput").ap())
    out = nc.dram_tensor("out", (GRAPHS, NODES, D), mybir.dt.float32, kind="ExternalOutput").ap()
    build(nc, *args, out)
    r = run_bass_kernel_spmd(nc, [arrays], core_ids=[0])
    return r.results[0]["out"]
```

```python
import numpy as np
import concourse.bass as bass
from concourse import mybir
from contextlib import ExitStack

GRAPHS, NODES, D, HID = 16, 512, 128, 512
P = 128
NB = NODES // P
HB = HID // P
PAIRS = GRAPHS // 2
JOINTS, NG, HID2 = 25, 5, 256
HB2 = HID2 // P
GI = NG * JOINTS
GROUPS = [list(range(25)), [0, 1, 2, 3, 4, 5, 6, 7, 8], [0, 9, 10, 11, 12, 13, 14],
          [6, 7, 8, 12, 13, 14], [3, 4, 5, 9, 10, 11]]
LN_EPS, RMS_EPS, DEG_EPS = 1e-5, 1e-6, 1e-5


def constant_columns():
    at, out = 0, {}
    for name, width in [("ident", P), ("spread", GI), ("gather", P), ("block", GI), ("member", JOINTS),
                        ("select", P), ("group", NG), ("own", 1)]:
        out[name] = (at, width)
        at += width
    return out, at


def shape_constants():
    cols, width = constant_columns()
    c = np.zeros((P, width), np.float32)

    def part(name):
        a, w = cols[name]
        return c[:, a:a + w]

    part("ident")[:] = np.eye(P)
    for g, idx in enumerate(GROUPS):
        for i in range(JOINTS):
            r = g * JOINTS + i
            part("spread")[i, r] = 1.0
            part("gather")[r, i] = 1.0
            part("block")[r, g * JOINTS:(g + 1) * JOINTS] = 1.0
            part("member")[r, idx] = 1.0
            part("group")[r, g] = 1.0
            if i in idx:
                part("select")[r, i] = 1.0
                part("own")[r, 0] = 1.0
    return c


def build(nc, x, adj, l0_eps, l0_w1, l0_b1, l0_rms, l0_w2, l0_b2, l1_w, l1_b, l2_w1, l2_b1, l2_w2,
          l2_b2, l2_fusion, l3_gamma, l3_beta, l3_self, l3_neigh, consts, out):
    fp32 = mybir.dt.float32
    ALU = mybir.AluOpType
    ACT = mybir.ActivationFunctionType
    AX = mybir.AxisListType
    cols, cwidth = constant_columns()

    ctx = ExitStack()
    with ctx:
        def sb(name, shape):
            return ctx.enter_context(nc.sbuf_tensor(name, shape, fp32))

        def sem(name):
            return ctx.enter_context(nc.semaphore(name))

        con = sb("con", [P, cwidth])
        w1 = sb("w1", [P, HID])
        w2 = sb("w2", [P, HB, D])
        b1c = sb("b1c", [P, HB])
        rmsc = sb("rmsc", [P, HB])
        b2 = sb("b2", [P, D])
        epsc = sb("epsc", [P, 1])
        wl1 = sb("wl1", [P, D])
        bl1 = sb("bl1", [P, D])
        gw1 = sb("gw1", [P, NG, HID2])
        gb1 = sb("gb1", [P, HB2, NG])
        ones = sb("ones", [P, 1])
        gw2 = sb("gw2", [P, NG, HB2, D])
        gb2 = sb("gb2", [P, D])
        fus = sb("fus", [P, 6 * NG])
        gammac = sb("gammac", [P, 1])
        betac = sb("betac", [P, 1])
        wself = sb("wself", [P, D])
        wneigh = sb("wneigh", [P, D])
        wsum = sb("wsum", [P, D])
        selw = sb("selw", [P, P])
        half = sb("half", [P, 24])
        ln_eps = sb("ln_eps", [P, 2 * NB])
        deg_eps = sb("deg_eps", [P, 2 * NB])
        zeros = sb("zeros", [P, 4 * NB])
        unit = sb("unit", [P, 2 * NB])
        spare = sb("spare", [1, 8])
        table = sb("table", [P, 1])

        def const(name, rows=P):
            a, w = cols[name]
            return con[0:rows, a:a + w]

        ident = const("ident")

        def per(name, shape):
            return [[sb(f"{name}_{q}{s}", shape) for s in range(2)] for q in range(2)]

        def two(name, shape):
            return [sb(f"{name}_{s}", shape) for s in range(2)]

        adjn_both = sb("adjn_both", [P, 2, NB, NODES])
        adjn = [adjn_both[:, s, :, :] for s in range(2)]
        adjT = per("adjT", [P, NB, NODES])
        xin = per("xin", [P, NB, D])
        x1b = per("x1b", [P, NB, D])
        x1s = per("x1s", [P, NB, D])
        ahatT = per("ahatT", [P, GI])
        ahatA = per("ahatA", [P, GI])
        sums = [sb(f"sums_{q}", [P, 2, 2, NB]) for q in range(2)]
        scal = [sb(f"scal_{q}", [P, 3, 2, NB]) for q in range(2)]
        ex = two("ex", [P, NB, D])
        xb = ex
        aggT = two("aggT", [P, NODES])
        hT = two("hT", [P, HB, NODES])
        sqT = two("sqT", [P, HB, NODES])
        ssq = two("ssq", [P, NB])
        rms = two("rms", [P, NB])
        r0 = two("r0", [P, NB, D])
        st0 = two("st0", [P, NB, 6])
        mv0 = two("mv0", [P, NB, 2])
        rs0 = two("rs0", [P, NB])
        x1 = two("x1", [P, NB, D])
        zer = sb("zer", [P, 2, 2, NB])
        zr = sb("zr", [P, 2, 2, NB])
        pw = sb("pw", [P, 3, 2, NB])
        deg = sb("deg", [P, 2])
        degz = sb("degz", [P, 6])
        dinv = sb("dinv", [P, 2])
        degj = two("degj", [P, JOINTS])
        bd = two("bd", [P, GI])
        yT = two("yT", [P, NODES])
        r1 = two("r1", [P, NB, D])
        st1 = two("st1", [P, NB, 6])
        mv1 = sb("mv1", [P, 2, NB, 2])
        vE = sb("vE", [P, 2, NB])
        rA = sb("rA", [P, 2, NB])
        vB = sb("vB", [P, 2, NB])
        tB = sb("tB", [P, 2, NB])
        rB = sb("rB", [P, 2, NB])
        rAB = sb("rAB", [P, 2, NB])
        vC = sb("vC", [P, 2, NB])
        rC = sb("rC", [P, 2, NB])
        x2 = two("x2", [P, D])
        ygT = sb("ygT", [P, 2, NG, JOINTS])
        hg = sb("hg", [P, HB2, NG, 2 * JOINTS])
        vgT = sb("vgT", [P, 2, NG, JOINTS])
        vg = sb("vg", [P, 2, D])
        og = sb("og", [P, 2, D])
        st2 = two("st2", [P, 6])
        x3 = two("x3", [P, NB, D])
        xh = two("xh", [P, NB, D])
        xnT = two("xnT", [P, NODES])
        vs = two("vs", [P, NB, D])
        tz = xh
        pre = two("pre", [P, NB, D])
        sp_abs = vs
        r3 = pre
        st3 = two("st3", [P, NB, 6])
        mv3 = two("mv3", [P, NB, 2])
        rs3 = two("rs3", [P, NB])
        yout = two("yout", [P, NB, D])

        bank = [ctx.enter_context(nc.psum_tensor(f"bank{i}", [P, 512], fp32)) for i in range(8)]

        def blocks(ap):
            return ap.rearrange("p (k n) -> p k n", k=NB)

        def flat4(tile):
            return tile[:, :, :, :].rearrange("p a s k -> p (a s k)")

        def wide(ap):
            return ap.rearrange("p k n -> p (k n)")

        con_in = sem("con_in")
        adj_half_in = sem("adj_half_in")
        eps_in = sem("eps_in")
        l0_in = sem("l0_in")
        weights_in = sem("weights_in")
        adj_in = [[sem(f"adj_in_{q}{s}") for s in range(2)] for q in range(2)]
        x_in = [[sem(f"x_in_{q}{s}") for s in range(2)] for q in range(2)]
        y_out = [sem(f"y_out_{s}") for s in range(2)]
        yj_ps = sem("yj_ps")
        yjT_sb = sem("yjT_sb")
        o1j_ps = sem("o1j_ps")
        r1j_sb = sem("r1j_sb")
        st1j_sb = sem("st1j_sb")
        mv1j_sb = sem("mv1j_sb")
        l1j_step = sem("l1j_step")
        rAj_sb = sem("rAj_sb")
        tr_ps = sem("tr_ps")
        agg_ps = sem("agg_ps")
        deg_ps = sem("deg_ps")
        bdT_ps = sem("bdT_ps")
        ahA_ps = sem("ahA_ps")
        hid_ps = sem("hid_ps")
        ssq_ps = sem("ssq_ps")
        rms_ps = sem("rms_ps")
        o0_ps = sem("o0_ps")
        y_ps = sem("y_ps")
        o1_ps = sem("o1_ps")
        yg_ps = sem("yg_ps")
        hg_ps = sem("hg_ps")
        vgT_ps = sem("vgT_ps")
        vg_ps = sem("vg_ps")
        og_ps = sem("og_ps")
        fused_ps = sem("fused_ps")
        xhT_rest_ps = sem("xhT_rest_ps")
        xhT_ps = sem("xhT_ps")
        v_rest_ps = sem("v_rest_ps")
        v_ps = sem("v_ps")
        z_ps = sem("z_ps")
        self_ps = sem("self_ps")
        adjT_sb = sem("adjT_sb")
        yT_sb = sem("yT_sb")
        aggT_sb = sem("aggT_sb")
        hid_sb = sem("hid_sb")
        sq_sb = sem("sq_sb")
        silu_sb = sem("silu_sb")
        ygT_sb = sem("ygT_sb")
        vgT_sb = sem("vgT_sb")
        vg_sb = sem("vg_sb")
        xnT_rest_sb = sem("xnT_rest_sb")
        xnT_sb = sem("xnT_sb")
        act_abs = sem("act_abs")
        act_exp = sem("act_exp")
        act_ln = sem("act_ln")
        fus_exp = sem("fus_exp")
        ones_sb = sem("ones_sb")
        setup_dve = sem("setup_dve")
        rowsum_sb = sem("rowsum_sb")
        r1_sb = sem("r1_sb")
        st1_sb = sem("st1_sb")
        mv1_sb = sem("mv1_sb")
        x2_sb = sem("x2_sb")
        deg_sb = sem("deg_sb")
        deg0_sb = sem("deg0_sb")
        sum0_sb = sem("sum0_sb")
        bd_sb = sem("bd_sb")
        ahT_sb = sem("ahT_sb")
        ahA_sb = sem("ahA_sb")
        ssq_sb = sem("ssq_sb")
        hgb_sb = sem("hgb_sb")
        hg_sb = sem("hg_sb")
        sq23_sb = sem("sq23_sb")
        sqsum = sem("sqsum")
        norm_sb = sem("norm_sb")
        ogb_sb = sem("ogb_sb")
        og_sb = sem("og_sb")
        r2_sb = sem("r2_sb")
        st2_sb = sem("st2_sb")
        mv2_sb = sem("mv2_sb")
        x3_sb = sem("x3_sb")
        xh_sb = sem("xh_sb")
        x3_rest_sb = sem("x3_rest_sb")
        xh_rest_sb = sem("xh_rest_sb")
        r0_sb = sem("r0_sb")
        st0_sb = sem("st0_sb")
        mv0_sb = sem("mv0_sb")
        x1_sb = sem("x1_sb")
        x1s_sb = sem("x1s_sb")
        vs_rest_sb = sem("vs_rest_sb")
        vs_sb = sem("vs_sb")
        tz_sb = sem("tz_sb")
        pre_sb = sem("pre_sb")
        sp_sb = sem("sp_sb")
        r3_sb = sem("r3_sb")
        st3_sb = sem("st3_sb")
        mv3_sb = sem("mv3_sb")
        y_sb = sem("y_sb")
        half_sb = sem("half_sb")
        stat_sb = sem("stat_sb")
        rA_sb = sem("rA_sb")
        dinv_sb = sem("dinv_sb")
        rs0_sb = sem("rs0_sb")
        rs3_sb = sem("rs3_sb")
        ex_sb = sem("ex_sb")
        xb_sb = sem("xb_sb")
        rms_sb = sem("rms_sb")
        sq01_sb = sem("sq01_sb")
        sq23_pool = sem("sq23_pool")
        rC13_sb = sem("rC13_sb")
        rC0_sb = sem("rC0_sb")
        l1_step = sem("l1_step")
        rest_step = sem("rest_step")
        joint_step = sem("joint_step")
        deg_step = sem("deg_step")
        stat_step = sem("stat_step")
        l0_step = sem("l0_step")
        l3_step = sem("l3_step")
        x1b_sb = sem("x1b_sb")

        L0_LOADS = 6
        LOADS = 7 + 3 * NG
        SETUP = 8
        EARLY = (2, 0)
        block = ctx.enter_context(nc.Block())

        def take_wait(n):
            nc.vector.memset(spare[:, n:n + 1], 0.0)

        def pairs_of(engine, body):
            body(0, 0, 0, True, False)
            body(1, 0, 1, True, True)
            with engine.Fori(0, (PAIRS - 2) // 2, 1) as i:
                body(2 * i + 2, i + 1, 0, True, True)
                body(2 * i + 3, i + 1, 1, True, True)
            body(PAIRS, PAIRS // 2, 0, False, True)

        def hidden_bank(s, k):
            return bank[(2, 3, 7)[(HB * s + k) % 3]]

        def rows_bank(one, s):
            return bank[6 + s if one else 3 + s]

        def values_bank(one, s):
            return bank[5 + s if one else (7, 2)[s]]

        def self_bank(one, s):
            return bank[(7, 2)[s] if one else 5 + s]

        def ending(t):
            return isinstance(t, int) and t == PAIRS

        @block.sync
        def _(sp):
            def row(vector, width):
                return vector.rearrange("(o d) -> o d", o=1).to_broadcast([P, width])

            l0_loads = [(w1[:, :], l0_w1), (b1c[:, :], l0_b1.rearrange("(k p) -> p k", p=P)),
                        (w2[:, :, :], l0_w2.rearrange("(k p) d -> p k d", p=P)),
                        (rmsc[:, :], l0_rms.rearrange("(k p) -> p k", p=P)),
                        (b2[:, :], row(l0_b2, D)), (bl1[:, :], row(l1_b, D))]
            loads = [(wl1[:, :], l1_w), (gw1[:, :, :], l2_w1.rearrange("g d h -> d g h"))]
            for g in range(NG):
                loads.append((gw2[:, g, :, :], l2_w2[g, :, :].rearrange("(k p) d -> p k d", p=P)))
                loads.append((gb1[:, :, g], l2_b1[g, :].rearrange("(k p) -> p k", p=P)))
                loads.append((gb2[g * JOINTS:(g + 1) * JOINTS, :], l2_b2[g:g + 1, :].to_broadcast([JOINTS, D])))
            loads += [(fus[:, 0:NG], row(l2_fusion, NG)), (wself[:, :], l3_self), (wneigh[:, :], l3_neigh),
                      (gammac[:, :], l3_gamma.rearrange("(p o) -> p o", o=1)),
                      (betac[:, :], l3_beta.rearrange("(p o) -> p o", o=1))]
            assert len(l0_loads) == L0_LOADS and len(loads) == LOADS

            def graph(tensor, g):
                if isinstance(g, int):
                    return tensor[g, :, :].rearrange("(k p) m -> p k m", p=P)
                return tensor[bass.ds(g, 1), :, :].rearrange("o (k p) m -> p (o k) m", p=P)

            def load(q, s, g):
                sp.dma_start(adjn[s][:, :, :], graph(adj, g)).then_inc(adj_in[q][s], 16)
                sp.dma_start(xin[q][s][:, :, :], graph(x, g)).then_inc(x_in[q][s], 16)

            sp.dma_start(con[:, :], consts).then_inc(con_in, 16)
            for half_in, at in ((adj_half_in, 0), (adj_in[0][0], NODES // 2)):
                sp.dma_start(adjn[0][:, :, at:at + NODES // 2],
                             graph(adj, 0)[:, :, at:at + NODES // 2]).then_inc(half_in, 16)
            sp.dma_start(xin[0][0][:, :, :], graph(x, 0)).then_inc(x_in[0][0], 16)
            with nc.allow_non_contiguous_dma(reason="vectors of at most 512 values, once"):
                sp.dma_start(epsc[:, :], row(l0_eps, 1)).then_inc(eps_in, 16)
                load(0, 1, 1)
                for dst, src in l0_loads:
                    sp.dma_start(dst, src).then_inc(l0_in, 16)
                for dst, src in loads:
                    sp.dma_start(dst, src).then_inc(weights_in, 16)
            sp.wait_ge(ahA_sb, 1)
            for s in range(2):
                load(1, s, 2 + s)

            def store(g, pair, s):
                sp.wait_ge(y_sb, 4 * (2 * pair + s + 1))
                sp.dma_start(graph(out, g), yout[s][:, :, :]).then_inc(y_out[s], 16)

            def load_and_store(t, q):
                graphs = [sp.snap(2 * t + k) for k in (0, 1, -4, -3)]
                sp.wait_ge(ahA_sb, t)
                for s in range(2):
                    load(q, s, graphs[s])
                for s in range(2):
                    store(graphs[2 + s], t - 2, s)

            with sp.Fori(0, (PAIRS - 2) // 2, 1) as i:
                load_and_store(2 * i + 2, 0)
                load_and_store(2 * i + 3, 1)
            for pair in (PAIRS - 2, PAIRS - 1):
                for s in range(2):
                    store(2 * pair + s, pair, s)
            for s in range(2):
                sp.wait_ge(y_out[s], 16 * PAIRS)

        @block.tensor
        def _(pe):
            mm = nc.tensor.matmul
            tp = nc.tensor.transpose
            pe.wait_ge(con_in, 16)

            def body(t, h, q, one, two_):
                u = t - 1
                three = not (isinstance(t, int) and t < 2)
                def a(s):
                    return 2 * t + s + 1

                def c(s):
                    return 2 * u + s + 1
                r = 1 - q

                def transpose_adjacency(s, j):
                    first = isinstance(t, int) and t == 0
                    if s == 0 and j == 0 and first:
                        pe.wait_ge(adj_half_in, 16)
                    if s == 0 and j == (NB // 2 if first else 0):
                        pe.wait_ge(adj_in[q][0], 16 * h + 16)
                    if s == 1 and j == 0:
                        pe.wait_ge(adj_in[q][1], 16 * h + 16)
                    if s or j >= 2:
                        pe.wait_ge(adjT_sb, 4 * (2 * t + s) + j - 1)
                    elif three:
                        pe.wait_ge(tz_sb, 2 * t - 3 + j)
                    elif two_ and j == 0:
                        pe.wait_ge(ahA_sb, t)
                    elif two_:
                        pe.wait_ge(norm_sb, 8 * t)
                    for i in range(NB):
                        last = tp(bank[j % 2][:, i * P:(i + 1) * P], adjn[s][:, i, j * P:(j + 1) * P], ident)
                    last.then_inc(tr_ps, 1)

                def neighbours1(s, j, lo=0, hi=NB, done=y_ps):
                    if j == 0:
                        pe.wait_ge(x1s_sb, c(s))
                    last = mm(bank[3 + s][:, lo * P:hi * P], x1s[r][s][:, j, :], adjT[r][s][:, j, lo * P:hi * P],
                              start=(j == 0), stop=(j == NB - 1))
                    if j == NB - 1:
                        last.then_inc(done, 1)

                def neighbours0(s, j):
                    if j == 0:
                        pe.wait_ge(adjT_sb, 4 * a(s))
                        pe.wait_ge(x_in[q][s], 16 * h + 16)
                        if s == 0 and two_:
                            pe.wait_ge(yT_sb, c(1))
                    mm(bank[4 if s == 0 else 0][:, :], xin[q][s][:, j, :], adjT[q][s][:, j, :],
                       start=(j == 0), stop=False)

                def self0(s):
                    pe.wait_ge(ex_sb, a(s))
                    b = bank[4 if s == 0 else 0]
                    for j in range(NB):
                        last = mm(b[:, j * P:(j + 1) * P], ex[s][:, j, :], ident, start=False,
                                  stop=(j == NB - 1), is_transpose=True)
                    last.then_inc(agg_ps, 1)

                def project1(s, lo=0, hi=NB, ready=yT_sb, done=o1_ps, past=0):
                    pe.wait_ge(ready, c(s) - past)
                    b = bank[7] if s == 0 else bank[5 if one else 2]
                    for i in range(lo, hi):
                        last = mm(b[:, i * P:(i + 1) * P], yT[s][:, i * P:(i + 1) * P], wl1[:, :],
                                  start=True, stop=True)
                    last.then_inc(done, 1)

                def hidden(s, k):
                    if k == 0:
                        pe.wait_ge(aggT_sb, a(s))
                        if s == 0 and three:
                            pe.wait_ge(pre_sb, 2 * t - 2)
                        if isinstance(t, int) and t == 0 and s == 0:
                            pe.wait_ge(l0_in, 16 * L0_LOADS)
                            pe.wait_ge(ones_sb, 1)
                    if HB * s + k >= 3:
                        pe.wait_ge(sq_sb, 8 * t + HB * s + k - 2)
                    elif HB * s + k == 2 and two_:
                        pe.wait_ge(r1_sb, c(0))
                    mm(hidden_bank(s, k)[:, :], w1[:, k * P:(k + 1) * P], aggT[s][:, :],
                       start=True, stop=True).then_inc(hid_ps, 1)

                def sum_squares(s):
                    pe.wait_ge(sqsum, a(s))
                    if s:
                        pe.wait_ge(ssq_sb, a(0))
                    for i in range(NB):
                        last = mm(bank[4][:, 2 * i:2 * i + 1], sqT[s][:, 0, i * P:(i + 1) * P], ones[:, :],
                                  start=True, stop=True)
                    last.then_inc(ssq_ps, 1)

                def spread_rms(s):
                    pe.wait_ge(rms_sb, a(s))
                    if s:
                        pe.wait_ge(norm_sb, 4 * a(0))
                    for i in range(NB):
                        last = tp(bank[1][:, i * P:(i + 1) * P], rms[s][:, i:i + 1].to_broadcast([P, P]), ident)
                    last.then_inc(rms_ps, 1)

                def project0(s, k):
                    b = bank[7 if s == 0 else 4]
                    pe.wait_ge(silu_sb, 4 * a(s) - 4 + k + 1)
                    for i in range(NB):
                        last = mm(b[:, i * P:(i + 1) * P], hT[s][:, k, i * P:(i + 1) * P], w2[:, k, :],
                                  start=(k == 0 and i == 0), stop=(k == HB - 1 and i == NB - 1))
                    if k == HB - 1:
                        last.then_inc(o0_ps, 1)

                def transpose_rest(s):
                    pe.wait_ge(xh_rest_sb, c(s))
                    if one and s == 0:
                        pe.wait_ge(ogb_sb, u + 1)
                    elif one:
                        pe.wait_ge(r0_sb, a(0))
                    for i in range(1, NB):
                        last = tp(rows_bank(one, s)[:, i * P:(i + 1) * P], xh[s][:, i, :], ident)
                    last.then_inc(xhT_rest_ps, 1)

                def transpose_joints():
                    for s in range(2):
                        pe.wait_ge(xh_sb, c(s))
                        if one and s == 0:
                            pe.wait_ge(vs_rest_sb, c(1))
                        tp(rows_bank(one, s)[:, 0:P], xh[s][:, 0, :], ident).then_inc(xhT_ps, 1)

                def values_rest():
                    for s in range(2):
                        pe.wait_ge(xnT_rest_sb, c(s))
                        if not one:
                            pe.wait_ge(r1_sb, c(s))
                        elif s == 0:
                            pe.wait_ge(r2_sb, c(1))
                        for i in range(1, NB):
                            last = mm(values_bank(one, s)[:, i * P:(i + 1) * P], xnT[s][:, i * P:(i + 1) * P],
                                      wneigh[:, :], start=True, stop=True)
                        last.then_inc(v_rest_ps, 1)

                def values_joints():
                    for s in range(2):
                        pe.wait_ge(xnT_sb, c(s))
                        if s == 0:
                            pe.wait_ge(vs_rest_sb, c(0))
                        mm(values_bank(one, s)[:, 0:P], xnT[s][:, 0:P], wneigh[:, :],
                           start=True, stop=True).then_inc(v_ps, 1)

                def neighbours3(s, js):
                    if js[0]:
                        pe.wait_ge(vs_rest_sb, c(s))
                        if one and s == 0:
                            pe.wait_ge(ahA_sb, t + 1)
                        elif one:
                            pe.wait_ge(norm_sb, 4 * a(1))
                    else:
                        pe.wait_ge(vs_sb, c(s))
                    for j in js:
                        for i in range(NB):
                            last = mm(bank[s][:, i * P:(i + 1) * P], adjT[r][s][:, j, i * P:(i + 1) * P],
                                      vs[s][:, j, :], start=(j == 1 and i == 0), stop=(j == 0 and i == NB - 1))
                    if js[0] == 0:
                        last.then_inc(z_ps, 1)

                def self3(s):
                    pe.wait_ge(xnT_sb, c(1))
                    if not one:
                        pe.wait_ge(r2_sb, c(1))
                    b = self_bank(one, s)
                    for i in range(NB):
                        last = mm(b[:, i * P:(i + 1) * P], xnT[s][:, i * P:(i + 1) * P], wsum[:, :],
                                  start=True, stop=True)
                    last.then_inc(self_ps, 1)

                early = EARLY if isinstance(t, int) and t == 1 else (0, 0)
                for s in range(2):
                    for j in range(early[s]):
                        transpose_adjacency(s, j)
                if not one:
                    for s in range(2):
                        for j in range(NB):
                            neighbours1(s, j, 0, 1, yj_ps)
                    for s in range(2):
                        guard_prev(pe, pre_sb, t, 1 + s)
                        project1(s, 0, 1, yjT_sb, o1j_ps, 2 * u)
                    for j in range(NB):
                        neighbours1(0, j, 1)
                for j in range(NB):
                    if one and two_:
                        neighbours1(0, j)
                for j in range(NB):
                    if one and early[0] + j < NB:
                        transpose_adjacency(0, early[0] + j)
                    if one and two_:
                        neighbours1(1, j)
                if isinstance(t, int) and t == 1:
                    pe.wait_ge(setup_dve, SETUP)
                if one and two_:
                    guard_prev(pe, pre_sb, t, 1)
                    project1(0)
                for j in range(NB):
                    if one:
                        if j >= early[1]:
                            transpose_adjacency(1, j)
                        neighbours0(0, j)
                    if one and two_ and j == 1:
                        project1(1)
                if one:
                    self0(0)
                    for j in range(NB):
                        neighbours0(1, j)
                    self0(1)
                    o = bank[1][0:GI, 0:2 * JOINTS]
                    mm(o, const("spread"), adjn_both[:, :, 0, 0:JOINTS], start=True, stop=False)
                    last = mm(o, const("spread"), ident[:, 0:JOINTS].rearrange("p (o j) -> p o j", o=1)
                              .to_broadcast([P, 2, JOINTS]), start=False, stop=True)
                    last.then_inc(deg_ps, 1)
                    for k in range(HB):
                        hidden(0, k)
                if two_:
                    pe.wait_ge(x2_sb, c(1))
                    for s in range(2):
                        last = mm(bank[6][:, s * GI:(s + 1) * GI], x2[s][:, :], ahatA[r][s][:, :],
                                  start=True, stop=True)
                    last.then_inc(yg_ps, 1)
                if not one:
                    project1(0, 1)
                    for j in range(NB):
                        neighbours1(1, j, 1)
                    project1(1, 1)
                if one:
                    hidden(1, 0)
                    hidden(1, 1)
                    hidden(1, 2)
                if two_:
                    pe.wait_ge(ygT_sb, u + 1)
                for k in range(HB2):
                    if one and k == 1:
                        sum_squares(0)
                    if two_:
                        for g in range(NG):
                            at = (k * NG + g) * 2 * JOINTS
                            last = mm(bank[5][:, at:at + 2 * JOINTS], gw1[:, g, k * P:(k + 1) * P],
                                      ygT[:, :, g, :], start=True, stop=True)
                if two_:
                    last.then_inc(hg_ps, 1)
                if one:
                    pe.wait_ge(bd_sb, t + 1)
                    pe.wait_ge(aggT_sb, a(1))
                    for g in range(2):
                        last = tp(bank[0][0:GI, P * g:P * g + GI], bd[g][0:GI, :], ident[0:GI, 0:GI])
                    last.then_inc(bdT_ps, 1)
                    hidden(1, 3)
                    spread_rms(0)
                if two_:
                    pe.wait_ge(hg_sb, u + 1)
                    for g in range(NG):
                        at = g * 2 * JOINTS
                        for k in range(HB2):
                            last = mm(bank[6][:, at:at + 2 * JOINTS], gw2[:, g, k, :], hg[:, k, g, :],
                                      start=(k == 0), stop=(k == HB2 - 1))
                    last.then_inc(vgT_ps, 1)
                if one:
                    pe.wait_ge(ahT_sb, t + 1)
                    for g in range(2):
                        last = mm(bank[0][:, P * g:P * g + GI], const("gather", GI), ahatT[q][g][0:GI, :],
                                  start=True, stop=True)
                    last.then_inc(ahA_ps, 1)
                if two_:
                    pe.wait_ge(vgT_sb, u + 1)
                    for s in range(2):
                        last = tp(bank[5][0:GI, s * D:(s + 1) * D], vgT[:, s, :, :].rearrange("p g i -> p (g i)"), ident)
                    last.then_inc(vg_ps, 1)
                if one:
                    project0(0, 0)
                    sum_squares(1)
                    project0(0, 1)
                if two_:
                    pe.wait_ge(vg_sb, u + 1)
                    for s in range(2):
                        last = mm(bank[6][0:GI, s * D:(s + 1) * D], ahatT[r][s][0:GI, :], vg[0:GI, s, :],
                                  start=True, stop=True)
                    last.then_inc(og_ps, 1)
                if one:
                    spread_rms(1)
                    project0(0, 2)
                    project0(0, 3)
                if two_:
                    if not one:
                        transpose_rest(0)
                    pe.wait_ge(og_sb, u + 1)
                    mm(bank[5][:, 0:2 * D], selw[0:GI, :], wide(og[0:GI, :, :]), start=True, stop=True).then_inc(fused_ps, 1)
                    if one:
                        transpose_rest(0)
                if one:
                    project0(1, 0)
                if two_:
                    transpose_rest(1)
                if one:
                    project0(1, 1)
                if two_:
                    values_rest()
                if one:
                    project0(1, 2)
                    project0(1, 3)
                if two_:
                    neighbours3(0, range(1, NB))
                    transpose_joints()
                    neighbours3(1, range(1, NB))
                    values_joints()
                    self3(0)
                    if one:
                        self3(1)
                    neighbours3(0, (0,))
                    if not one:
                        self3(1)
                    neighbours3(1, (0,))

            def guard_prev(eng, what, t, k):
                if isinstance(t, int) and t == 1:
                    return
                eng.wait_ge(what, 2 * t - 4 + k)

            pairs_of(pe, body)

        @block.scalar
        def _(act):
            A = nc.scalar.activation
            act.wait_ge(half_sb, 5)
            A(table[:, :], zeros[:, 0:1], ACT.Silu)

            def body(t, h, q, one, two_):
                u = t - 1
                three = not (isinstance(t, int) and t < 2)

                def a(s):
                    return 2 * t + s + 1

                def c(s):
                    return 2 * u + s + 1

                def adjacency(s, js=range(NB)):
                    for j in js:
                        act.wait_ge(tr_ps, 4 * (2 * t + s) + j + 1)
                        A(adjT[q][s][:, j, :], bank[j % 2][:, :], ACT.Identity,
                          accum_out=sums[q][:, 1, s, j:j + 1]).then_inc(adjT_sb, 1)

                def neighbours1(s, lo=0, hi=NB, ready=y_ps, done=yT_sb, past=0):
                    act.wait_ge(ready, c(s) - past)
                    A(yT[s][:, lo * P:hi * P], bank[3 + s][:, lo * P:hi * P], ACT.Identity).then_inc(done, 1)

                def neighbours0(s):
                    act.wait_ge(agg_ps, a(s))
                    A(aggT[s][:, :], bank[4 if s == 0 else 0][:, :], ACT.Identity).then_inc(aggT_sb, 1)

                def softplus_abs(p, slots=(0, 1)):
                    for s in slots:
                        act.wait_ge(pre_sb, 2 * p + s + 1)
                        A(wide(sp_abs[s][:, :, :]), wide(pre[s][:, :, :]), ACT.Abs).then_inc(act_abs, 1)

                def softplus_exp(p, slots=(0, 1)):
                    for s in slots:
                        act.wait_ge(act_abs, 2 * p + s + 1)
                        e = wide(sp_abs[s][:, :, :])
                        A(e, e, ACT.Exp, scale=-1.0).then_inc(act_exp, 1)

                def softplus_ln(p, slots=(0, 1)):
                    for s in slots:
                        act.wait_ge(act_exp, 2 * p + s + 1)
                        e = wide(sp_abs[s][:, :, :])
                        A(e, e, ACT.Ln, bias=1.0).then_inc(act_ln, 1)

                def hidden(s):
                    if isinstance(t, int) and t == 0 and s == 0:
                        act.wait_ge(l0_in, 16 * L0_LOADS)
                    for k in range(HB):
                        act.wait_ge(hid_ps, 4 * (2 * t + s) + k + 1)
                        A(hT[s][:, k, :], hidden_bank(s, k)[:, :], ACT.Identity, bias=b1c[:, k:k + 1]).then_inc(hid_sb, 1)
                        A(sqT[s][:, k, :], hidden_bank(s, k)[:, :], ACT.Square, bias=b1c[:, k:k + 1]).then_inc(sq_sb, 1)

                if not one:
                    for s in range(2):
                        neighbours1(s, 0, 1, yj_ps, yjT_sb, 2 * u)
                if three:
                    softplus_abs(t - 2)
                early = EARLY if isinstance(t, int) and t == 1 else (0, 0)
                for s in range(2):
                    adjacency(s, range(early[s]))
                if one and two_:
                    neighbours1(0)
                if one:
                    adjacency(0, range(early[0], NB))
                if one and two_:
                    neighbours1(1)
                if three:
                    softplus_exp(t - 2)
                if not one:
                    neighbours1(0, 1)
                if one:
                    adjacency(1, range(early[1], NB))
                    neighbours0(0)
                if three and one:
                    softplus_ln(t - 2)
                if one:
                    neighbours0(1)
                    hidden(0)
                if two_:
                    act.wait_ge(yg_ps, u + 1)
                    A(ygT[:, :, :, :].rearrange("p s g i -> p (s g i)"), bank[6][:, 0:2 * GI], ACT.Identity).then_inc(ygT_sb, 1)
                if not one:
                    softplus_ln(t - 2)
                    neighbours1(1, 1)
                if one:
                    hidden(1)

                def silu(s, ks=range(HB)):
                    for k in ks:
                        act.wait_ge(norm_sb, 4 * (2 * t + s) + k + 1)
                        A(hT[s][:, k, :], hT[s][:, k, :], ACT.Silu, scale=rmsc[:, k:k + 1]).then_inc(silu_sb, 1)

                if one:
                    silu(0)
                    silu(1, (0, 1))
                if two_:
                    for s in range(2):
                        act.wait_ge(xhT_rest_ps, c(s))
                        A(xnT[s][:, P:], rows_bank(one, s)[:, P:], ACT.Identity, bias=betac[:, 0:1],
                          scale=gammac[:, 0:1]).then_inc(xnT_rest_sb, 1)
                if one:
                    silu(1, (2, 3))
                if two_:
                    for s in range(2):
                        act.wait_ge(xhT_ps, c(s))
                        A(xnT[s][:, 0:P], rows_bank(one, s)[:, 0:P], ACT.Identity, bias=betac[:, 0:1],
                          scale=gammac[:, 0:1]).then_inc(xnT_sb, 1)
                if ending(t):
                    act.wait_ge(half_sb, 5)
                    A(table[:, :], zeros[:, 0:1], ACT.Exp)
                    for s in range(2):
                        softplus_abs(t - 1, (s,))
                        softplus_exp(t - 1, (s,))
                    softplus_ln(t - 1)

                if isinstance(t, int) and t == 0:
                    act.wait_ge(setup_dve, 2)
                    A(fus[:, 15:20], fus[:, 10:15], ACT.Exp).then_inc(fus_exp, 1)

            pairs_of(act, body)

        @block.vector
        def _(dve):
            V = nc.vector

            V.memset(ones[:, :], 1.0).then_inc(ones_sb, 1)
            dve.wait_ge(con_in, 16)

            def weights():
                dve.wait_ge(weights_in, 16 * LOADS)
                V.reduce_max(fus[:, 5:6], fus[:, 0:NG], AX.X).then_inc(setup_dve, 1)
                dve.wait_ge(setup_dve, 1)
                V.tensor_scalar(fus[:, 10:15], fus[:, 0:NG], fus[:, 5:6], None, ALU.subtract).then_inc(setup_dve, 1)
                V.tensor_tensor(wsum[:, :], wself[:, :], wneigh[:, :], ALU.add).then_inc(setup_dve, 1)
                dve.wait_ge(fus_exp, 1)
                V.tensor_reduce(fus[:, 6:7], fus[:, 15:20], AX.X, ALU.add).then_inc(setup_dve, 1)
                V.tensor_tensor(fus[:, 20:25], fus[:, 15:20], const("group"), ALU.mult).then_inc(setup_dve, 1)
                dve.wait_ge(setup_dve, 5)
                V.reciprocal(fus[:, 7:8], fus[:, 6:7]).then_inc(setup_dve, 1)
                V.tensor_reduce(fus[:, 8:9], fus[:, 20:25], AX.X, ALU.add).then_inc(setup_dve, 1)
                dve.wait_ge(setup_dve, 7)
                V.tensor_scalar(selw[:, :], const("select"), fus[:, 7:8], fus[:, 8:9], ALU.mult, ALU.mult).then_inc(setup_dve, 1)

            def body(t, h, q, one, two_):
                u = t - 1
                three = not (isinstance(t, int) and t < 2)
                r = 1 - q

                def a(s):
                    return 2 * t + s + 1

                def c(s):
                    return 2 * u + s + 1

                if one:
                    for s in range(2):
                        if isinstance(t, int) and t == 0:
                            dve.wait_ge(adj_half_in, 16)
                        dve.wait_ge(adj_in[q][s], 16 * h + 16)
                        V.tensor_reduce(sums[q][:, 0, s, :], adjn[s][:, :, :], AX.X, ALU.add).then_inc(rowsum_sb, 1)
                def l1_residual(s, lo=0, hi=NB, ready=o1_ps, done=r1_sb, past=0):
                    dve.wait_ge(ready, c(s) - past)
                    dve.wait_ge(x1b_sb, c(s))
                    b = bank[7] if s == 0 else bank[5 if one else 2]
                    for i in range(lo, hi):
                        last = V.scalar_tensor_tensor(
                            out=r1[s][:, i, :], in0=b[:, i * P:(i + 1) * P],
                            scalar=scal[r][:, 0, s, i:i + 1], in1=x1b[r][s][:, i, :], op0=ALU.mult, op1=ALU.add)
                    last.then_inc(done, 1)

                def l1_stats(lo=0, hi=NB, ready=r1_sb, stats=st1_sb, done=mv1_sb, past=0, slots=(0, 1)):
                    for s in slots:
                        dve.wait_ge(ready, c(s) - past)
                        for i in range(lo, hi):
                            last = V.bn_stats(st1[s][:, i, :], r1[s][:, i, :])
                        last.then_inc(stats, 1)
                    for s in slots:
                        dve.wait_ge(stats, c(s) - past)
                        take_wait(s)
                        for i in range(lo, hi):
                            last = V.bn_aggr(mv1[:, s, i, :], st1[s][:, i, :])
                        last.then_inc(done, 1)

                def joints_input(scale, stats, past=0):
                    for s in range(2):
                        dve.wait_ge(scale, u + 1 - past)
                        dve.wait_ge(stats, c(s) - 2 * past)
                        V.tensor_scalar(x2[s][:, :], r1[s][:, 0, :], mv1[:, s, 0, 0:1], rA[:, s, 0:1],
                                        ALU.subtract, ALU.mult).then_inc(x2_sb, 1)

                if one and two_:
                    l1_residual(0)
                    l1_residual(1)
                    l1_stats()
                elif two_:
                    for s in range(2):
                        l1_residual(s, 0, 1, o1j_ps, r1j_sb, 2 * u)
                    l1_stats(0, 1, r1j_sb, st1j_sb, mv1j_sb, 2 * u)

                def softplus_linear(p, s):
                    dve.wait_ge(act_abs, 2 * p + s + 1)
                    V.scalar_tensor_tensor(out=pre[s][:, :, :], in0=pre[s][:, :, :], scalar=0.0,
                                           in1=x3[s][:, :, :], op0=ALU.max, op1=ALU.add).then_inc(sp_sb, 1)

                def softplus_sum(p, s):
                    n = 2 * p + s + 1
                    dve.wait_ge(act_ln, n)
                    dve.wait_ge(sp_sb, n)
                    V.tensor_tensor(r3[s][:, :, :], pre[s][:, :, :], sp_abs[s][:, :, :], ALU.add).then_inc(r3_sb, 1)

                def softplus_stats(p, s):
                    n = 2 * p + s + 1
                    dve.wait_ge(r3_sb, n)
                    for i in range(NB):
                        last = V.bn_stats(st3[s][:, i, :], r3[s][:, i, :])
                    last.then_inc(st3_sb, 1)
                    dve.wait_ge(st3_sb, n)
                    take_wait(6 + s)
                    for i in range(NB):
                        last = V.bn_aggr(mv3[s][:, i, :], st3[s][:, i, :])
                    last.then_inc(mv3_sb, 1)

                def result(p, s):
                    dve.wait_ge(rs3_sb, 2 * p + s + 1)
                    if not (isinstance(p, int) and p == 0):
                        dve.wait_ge(y_out[s], 16 * p)
                    for i in range(NB):
                        V.tensor_scalar(yout[s][:, i, :], r3[s][:, i, :], mv3[s][:, i, 0:1], rs3[s][:, i:i + 1],
                                        ALU.subtract, ALU.mult).then_inc(y_sb, 1)

                def l0_residual(s):
                    dve.wait_ge(o0_ps, a(s))
                    dve.wait_ge(xb_sb, a(s))
                    V.tensor_tensor(wide(r0[s][:, :, :]), bank[7 if s == 0 else 4][:, :], wide(xb[s][:, :, :]),
                                    ALU.add).then_inc(r0_sb, 1)

                def mean_square(s):
                    dve.wait_ge(ssq_ps, a(s))
                    V.tensor_scalar(ssq[s][:, :], bank[4][:, 0:2 * NB].rearrange("p (k o) -> p k o", o=2)[:, :, 0],
                                    1.0 / HID, RMS_EPS, ALU.mult, ALU.add).then_inc(ssq_sb, 1)

                def add_squares(s):
                    if s == 0:
                        dve.wait_ge(sq_sb, 4 * a(s))
                        V.tensor_tensor(sqT[s][:, 2, :], sqT[s][:, 2, :], sqT[s][:, 3, :], ALU.add).then_inc(sq23_sb, 1)
                        dve.wait_ge(sq23_sb, t + 1)
                    else:
                        dve.wait_ge(sq23_pool, t + 1)
                    dve.wait_ge(sq01_sb, a(s))
                    V.tensor_tensor(sqT[s][:, 0, :], sqT[s][:, 0, :], sqT[s][:, 2, :], ALU.add).then_inc(sqsum, 1)

                def normalise(s, k):
                    if k == 0:
                        dve.wait_ge(rms_ps, a(s))
                        dve.wait_ge(hid_sb, 4 * a(s))
                    V.tensor_tensor(hT[s][:, k, :], hT[s][:, k, :], bank[1][:, :], ALU.mult).then_inc(norm_sb, 1)

                def l2_norm(s, lo, hi, x3_done, xh_done):
                    for i in range(lo, hi):
                        last = V.tensor_scalar(x3[s][:, i, :], r1[s][:, i, :], mv1[:, s, i, 0:1], rAB[:, s, i:i + 1],
                                               ALU.subtract, ALU.mult)
                    last.then_inc(x3_done, 1)
                    dve.wait_ge(x3_done, c(s))
                    V.tensor_tensor(xh[s][:, lo:hi, :], x3[s][:, lo:hi, :],
                                    rC[:, s, lo:hi].rearrange("p (k o) -> p k o", o=1).to_broadcast([P, hi - lo, D]),
                                    ALU.mult).then_inc(xh_done, 1)

                def l2_norm_rest(s):
                    dve.wait_ge(rC13_sb, u + 1)
                    l2_norm(s, 1, NB, x3_rest_sb, xh_rest_sb)

                if three and one:
                    softplus_linear(t - 2, 0)
                    softplus_sum(t - 2, 0)
                    softplus_stats(t - 2, 0)
                if one:
                    dve.wait_ge(deg_ps, t + 1)
                    for s in range(2):
                        V.tensor_tensor_reduce(out=degj[s][0:GI, :], in0=bank[1][0:GI, s * JOINTS:(s + 1) * JOINTS],
                                               in1=const("member", GI), scale=1.0, scalar=0.0, op0=ALU.mult,
                                               op1=ALU.add, accum_out=deg[0:GI, s:s + 1]).then_inc(deg_sb, 1)
                    dve.wait_ge(deg_sb, 2 * t + 2)
                    V.tensor_scalar(degz[0:GI, 0:2], deg[0:GI, :], 0.0, None, ALU.is_equal).then_inc(deg0_sb, 1)
                    dve.wait_ge(rowsum_sb, 2 * t + 2)
                    dve.wait_ge(adjT_sb, 8 * t + 8)
                    V.tensor_scalar(flat4(zer), flat4(sums[q]), 0.0, None, ALU.is_equal).then_inc(sum0_sb, 1)
                if one and two_:
                    joints_input(rA_sb, mv1_sb)
                elif two_:
                    joints_input(rAj_sb, mv1j_sb, u)
                if ending(t):
                    softplus_linear(t - 2, 0)
                    softplus_linear(t - 2, 1)
                    l1_residual(0, 1)
                    l1_stats(1, slots=(0,))
                    softplus_sum(t - 2, 0)
                    softplus_sum(t - 2, 1)
                    l1_residual(1, 1)
                    l1_stats(1, slots=(1,))
                if three and one:
                    softplus_linear(t - 2, 1)
                    softplus_sum(t - 2, 1)
                    softplus_stats(t - 2, 1)
                if one:
                    dve.wait_ge(dinv_sb, t + 1)
                    for s in range(2):
                        last = V.scalar_tensor_tensor(
                            out=bd[s][0:GI, :].rearrange("p (g j) -> p g j", g=NG),
                            in0=bank[1][0:GI, s * JOINTS:(s + 1) * JOINTS].rearrange("p (o j) -> p o j", o=1)
                            .to_broadcast([GI, NG, JOINTS]),
                            scalar=dinv[0:GI, s:s + 1],
                            in1=const("block", GI).rearrange("p (g j) -> p g j", g=NG), op0=ALU.mult, op1=ALU.mult)
                    last.then_inc(bd_sb, 1)
                    add_squares(0)
                if three and one:
                    result(t - 2, 0)
                if one:
                    mean_square(0)
                if three and one:
                    result(t - 2, 1)
                if two_:
                    dve.wait_ge(hg_ps, u + 1)
                    n = HB2 * NG
                    hflat = hg[:, :, :, :].rearrange("p k g i -> p (k g) i")
                    V.tensor_tensor(hflat, bank[5][:, 0:n * 2 * JOINTS].rearrange("p (n i) -> p n i", n=n),
                                    gb1[:, :, :].rearrange("p k (g o) -> p (k g) o", o=1).to_broadcast([P, n, 2 * JOINTS]),
                                    ALU.add).then_inc(hgb_sb, 1)
                    dve.wait_ge(hgb_sb, u + 1)
                    V.tensor_scalar(hflat, hflat, 0.0, None, ALU.max).then_inc(hg_sb, 1)
                if one:
                    dve.wait_ge(bdT_ps, t + 1)
                    for s in range(2):
                        last = V.tensor_scalar(ahatT[q][s][0:GI, :], bank[0][0:GI, P * s:P * s + GI],
                                               dinv[0:GI, s:s + 1], None, ALU.mult)
                    last.then_inc(ahT_sb, 1)
                    for k in range(HB - 1):
                        normalise(0, k)
                if ending(t):
                    softplus_stats(t - 2, 0)
                if two_:
                    dve.wait_ge(vgT_ps, u + 1)
                    V.tensor_copy(vgT[:, :, :, :].rearrange("p s g i -> p g s i"),
                                  bank[6][:, 0:2 * GI].rearrange("p (g s i) -> p g s i", g=NG, s=2)).then_inc(vgT_sb, 1)
                if one:
                    normalise(0, HB - 1)
                    add_squares(1)
                    dve.wait_ge(ahA_ps, t + 1)
                    for s in range(2):
                        last = V.tensor_copy(ahatA[q][s][:, :], bank[0][:, P * s:P * s + GI])
                    last.then_inc(ahA_sb, 1)
                if two_:
                    dve.wait_ge(vg_ps, u + 1)
                    V.tensor_copy(wide(vg[0:GI, :, :]), bank[5][0:GI, 0:2 * D]).then_inc(vg_sb, 1)
                if one:
                    mean_square(1)
                if two_:
                    l2_norm_rest(0)
                if two_:
                    dve.wait_ge(og_ps, u + 1)
                    V.tensor_tensor(og[0:GI, :, :], bank[6][0:GI, 0:2 * D].rearrange("p (s d) -> p s d", s=2),
                                    gb2[0:GI, :].rearrange("p (o d) -> p o d", o=1).to_broadcast([GI, 2, D]),
                                    ALU.add).then_inc(ogb_sb, 1)
                    dve.wait_ge(ogb_sb, u + 1)
                    V.tensor_scalar(og[0:GI, :, :], og[0:GI, :, :], 0.0, None, ALU.max).then_inc(og_sb, 1)
                if one:
                    normalise(1, 0)
                    normalise(1, 1)
                if two_:
                    l2_norm_rest(1)
                if one:
                    l0_residual(0)
                    normalise(1, 2)
                def l3_values(s, lo, hi, ready, done):
                    dve.wait_ge(ready, c(s))
                    V.tensor_tensor(vs[s][:, lo:hi, :], blocks(values_bank(one, s)[:, :])[:, lo:hi, :],
                                    scal[r][:, 1, s, lo:hi].rearrange("p (k o) -> p k o", o=1).to_broadcast([P, hi - lo, D]),
                                    ALU.mult).then_inc(done, 1)

                if two_:
                    dve.wait_ge(fused_ps, u + 1)
                    for s in range(2):
                        V.tensor_tensor(r1[s][:, 0, :], bank[5][:, s * D:(s + 1) * D], x2[s][:, :],
                                        ALU.add).then_inc(r2_sb, 1)
                    for s in range(2):
                        dve.wait_ge(r2_sb, c(s))
                        V.bn_stats(st2[s][:, :], r1[s][:, 0, :]).then_inc(st2_sb, 1)
                    dve.wait_ge(l1_step, 3 * u + 2)
                    for s in range(2):
                        dve.wait_ge(st2_sb, c(s))
                        take_wait(2 + s)
                        V.bn_aggr(mv1[:, s, 0, :], st2[s][:, :]).then_inc(mv2_sb, 1)
                if one:
                    normalise(1, HB - 1)
                def l0_stats(s):
                    dve.wait_ge(r0_sb, a(s))
                    for i in range(NB):
                        last = V.bn_stats(st0[s][:, i, :], r0[s][:, i, :])
                    last.then_inc(st0_sb, 1)
                    dve.wait_ge(st0_sb, a(s))
                    take_wait(4 + s)
                    for i in range(NB):
                        last = V.bn_aggr(mv0[s][:, i, :], st0[s][:, i, :])
                    last.then_inc(mv0_sb, 1)

                def l0_norm(s):
                    dve.wait_ge(rs0_sb, a(s))
                    for i in range(NB):
                        last = V.tensor_scalar(x1[s][:, i, :], r0[s][:, i, :], mv0[s][:, i, 0:1], rs0[s][:, i:i + 1],
                                               ALU.subtract, ALU.mult)
                    last.then_inc(x1_sb, 1)
                    dve.wait_ge(x1_sb, a(s))
                    dve.wait_ge(stat_sb, t + 1)
                    V.tensor_tensor(x1s[q][s][:, :, :], x1[s][:, :, :],
                                    scal[q][:, 0, s, :].rearrange("p (k o) -> p k o", o=1).to_broadcast([P, NB, D]),
                                    ALU.mult).then_inc(x1s_sb, 1)

                if two_:
                    for s in range(2):
                        l3_values(s, 1, NB, v_rest_ps, vs_rest_sb)
                if one:
                    l0_stats(0)
                if two_:
                    dve.wait_ge(rC0_sb, u + 1)
                    for s in range(2):
                        l2_norm(s, 0, 1, x3_sb, xh_sb)
                if ending(t):
                    result(t - 2, 0)
                    softplus_stats(t - 2, 1)
                if one:
                    l0_residual(1)
                    l0_stats(1)
                if two_:
                    for s in range(2):
                        l3_values(s, 0, 1, v_ps, vs_sb)
                if ending(t):
                    result(t - 2, 1)
                for s in range(2):
                    if one:
                        l0_norm(s)
                    if two_:
                        dve.wait_ge(z_ps, c(s))
                        V.tensor_tensor(tz[s][:, :, :], blocks(bank[s][:, :]),
                                        scal[r][:, 2, s, :].rearrange("p (k o) -> p k o", o=1).to_broadcast([P, NB, D]),
                                        ALU.mult).then_inc(tz_sb, 1)
                        dve.wait_ge(self_ps, c(s))
                        dve.wait_ge(tz_sb, c(s))
                        V.tensor_tensor(pre[s][:, :, :], blocks(self_bank(one, s)[:, :]), tz[s][:, :, :],
                                        ALU.add).then_inc(pre_sb, 1)
                if ending(t):
                    for s in range(2):
                        softplus_linear(t - 1, s)
                    for s in range(2):
                        softplus_sum(t - 1, s)
                        softplus_stats(t - 1, s)
                    for s in range(2):
                        result(t - 1, s)

                if isinstance(t, int) and t == 0:
                    weights()

            pairs_of(dve, body)

        @block.gpsimd
        def _(pool):
            G = nc.gpsimd
            for tile, value in ((half, -0.5), (ln_eps, LN_EPS), (deg_eps, DEG_EPS), (zeros, 0.0), (unit, 1.0)):
                G.memset(tile[:, :], value).then_inc(half_sb, 1)
            pool.wait_ge(half_sb, 5)
            pool.wait_ge(con_in, 16)
            pool.wait_ge(eps_in, 16)

            def slots(tile):
                return tile[:, 0:2 * NB].rearrange("p (s k) -> p s k", s=2)

            def rsqrt(out_, in_, n, what):
                G.tensor_tensor(out_, in_, half[0:in_.shape[0], 0:n], ALU.pow).then_inc(what, 1)

            def body(t, h, q, one, two_):
                u = t - 1
                three = not (isinstance(t, int) and t < 2)

                def a(s):
                    return 2 * t + s + 1

                def c(s):
                    return 2 * u + s + 1

                def l0_input(s):
                    if isinstance(t, int) and t == 0 and s == 0:
                        pool.wait_ge(l0_in, 16 * L0_LOADS)
                    pool.wait_ge(agg_ps, a(s))
                    G.tensor_tensor(xb[s][:, :, :], xin[q][s][:, :, :],
                                    b2[:, :].rearrange("p (o d) -> p o d", o=1).to_broadcast([P, NB, D]),
                                    ALU.add).then_inc(xb_sb, 1)

                def last_scale(p, s):
                    n = 2 * p + s + 1
                    pool.wait_ge(mv3_sb, n)
                    G.tensor_tensor(mv3[s][:, :, 1], mv3[s][:, :, 1], ln_eps[:, 0:NB], ALU.add).then_inc(l3_step, 1)
                    pool.wait_ge(l3_step, n)
                    rsqrt(rs3[s][:, :], mv3[s][:, :, 1], NB, rs3_sb)

                if one:
                    for s in range(2):
                        pool.wait_ge(x_in[q][s], 16 * h + 16)
                        if two_:
                            pool.wait_ge(r0_sb, 2 * t - 1 + s)
                        G.tensor_tensor(wide(ex[s][:, :, :]), wide(xin[q][s][:, :, :]),
                                        epsc[:, 0:1].to_broadcast([P, NB * D]), ALU.mult).then_inc(ex_sb, 1)
                if not one:
                    pool.wait_ge(mv1j_sb, 2)
                    pool.wait_ge(xh_sb, c(1) - 2)
                    G.tensor_tensor(vE[:, :, 0:1], mv1[:, :, 0:1, 1], slots(ln_eps)[:, :, 0:1], ALU.add).then_inc(l1j_step, 1)
                    pool.wait_ge(l1j_step, 1)
                    G.tensor_tensor(rA[:, :, 0:1], vE[:, :, 0:1], slots(half)[:, :, 0:1], ALU.pow).then_inc(rAj_sb, 1)
                if two_:
                    lo = 0 if one else 1
                    b = (slice(None), slice(None), slice(lo, NB))
                    pool.wait_ge(mv1_sb, c(1))
                    if one and not (isinstance(t, int) and t == 1):
                        pool.wait_ge(xh_sb, c(1) - 2)
                    v = mv1[:, :, lo:NB, 1]
                    G.tensor_tensor(vE[b], v, slots(ln_eps)[:, :, lo:NB], ALU.add).then_inc(l1_step, 1)
                    pool.wait_ge(l1_step, 3 * u + 1)
                    G.tensor_tensor(rA[b], vE[b], slots(half)[:, :, lo:NB], ALU.pow).then_inc(rA_sb, 1)
                    pool.wait_ge(rA_sb, u + 1)
                    G.tensor_tensor(tB[b], v, rA[b], ALU.mult).then_inc(l1_step, 1)
                    pool.wait_ge(l1_step, 3 * u + 2)
                    G.tensor_tensor(vB[b], tB[b], rA[b], ALU.mult).then_inc(l1_step, 1)
                if one:
                    l0_input(0)
                    pool.wait_ge(deg0_sb, t + 1)
                    d = degz[0:GI, :]
                    G.tensor_tensor(d[:, 2:4], deg[0:GI, :], d[:, 0:2], ALU.add).then_inc(deg_step, 1)
                    pool.wait_ge(deg_step, 4 * t + 1)
                    rsqrt(d[:, 4:6], d[:, 2:4], 2, deg_step)
                    G.tensor_tensor(d[:, 0:2], unit[0:GI, 0:2], d[:, 0:2], ALU.subtract).then_inc(deg_step, 1)
                    pool.wait_ge(deg_step, 4 * t + 3)
                    G.tensor_tensor(d[:, 0:2], d[:, 0:2], d[:, 4:6], ALU.mult).then_inc(deg_step, 1)
                    pool.wait_ge(deg_step, 4 * t + 4)
                    G.tensor_tensor(dinv[0:GI, :], d[:, 0:2], const("own", GI).to_broadcast([GI, 2]), ALU.mult).then_inc(dinv_sb, 1)

                def add_squares(s):
                    pool.wait_ge(sq_sb, 4 * (2 * t + s) + 2)
                    G.tensor_tensor(sqT[s][:, 0, :], sqT[s][:, 0, :], sqT[s][:, 1, :], ALU.add).then_inc(sq01_sb, 1)

                def inverse_rms(s):
                    pool.wait_ge(ssq_sb, a(s))
                    rsqrt(rms[s][:, :], ssq[s][:, :], NB, rms_sb)

                def l2_scale(lo, hi, var, step, at):
                    b = (slice(None), slice(None), slice(lo, hi))
                    eps = slots(ln_eps)[:, :, 0:hi - lo]
                    power = slots(half)[:, :, 0:hi - lo]
                    G.tensor_tensor(tB[b], var, eps, ALU.add).then_inc(step, 1)
                    pool.wait_ge(step, at + 1)
                    G.tensor_tensor(rB[b], tB[b], power, ALU.pow).then_inc(step, 1)

                def l3_scale(lo, hi, var, step, at, done):
                    b = (slice(None), slice(None), slice(lo, hi))
                    eps = slots(ln_eps)[:, :, 0:hi - lo]
                    power = slots(half)[:, :, 0:hi - lo]
                    pool.wait_ge(step, at + 2)
                    G.tensor_tensor(vC[b], var, rB[b], ALU.mult).then_inc(step, 1)
                    pool.wait_ge(step, at + 3)
                    G.tensor_tensor(vC[b], vC[b], rB[b], ALU.mult).then_inc(step, 1)
                    pool.wait_ge(step, at + 4)
                    G.tensor_tensor(vC[b], vC[b], eps, ALU.add).then_inc(step, 1)
                    other = rA[b] if lo else slots(unit)[:, :, 0:hi]
                    G.tensor_tensor(rAB[b], other, rB[b], ALU.mult).then_inc(step, 1)
                    pool.wait_ge(step, at + 6)
                    G.tensor_tensor(rC[b], vC[b], power, ALU.pow).then_inc(done, 1)

                if one:
                    add_squares(0)
                if three and one:
                    last_scale(t - 2, 0)
                if three and one:
                    last_scale(t - 2, 1)
                if one:
                    inverse_rms(0)
                    add_squares(1)
                if two_:
                    pool.wait_ge(l1_step, 3 * u + 3)
                    l2_scale(1, NB, vB[:, :, 1:NB], rest_step, 6 * u)
                if one:
                    pool.wait_ge(sq_sb, 8 * t + 8)
                    G.tensor_tensor(sqT[1][:, 2, :], sqT[1][:, 2, :], sqT[1][:, 3, :], ALU.add).then_inc(sq23_pool, 1)
                if two_:
                    l3_scale(1, NB, vB[:, :, 1:NB], rest_step, 6 * u, rC13_sb)
                if ending(t):
                    last_scale(t - 2, 0)
                if one:
                    inverse_rms(1)
                    l0_input(1)
                    pool.wait_ge(sum0_sb, t + 1)
                    if two_ and not (isinstance(t, int) and t == 1):
                        pool.wait_ge(tz_sb, 2 * t - 2)
                    S = sums[q]
                    G.tensor_tensor(pw[:, 0, :, :], S[:, 0, :, :], slots(deg_eps), ALU.add).then_inc(stat_step, 1)
                    G.tensor_tensor(pw[:, 1:3, :, :], S[:, :, :, :], zer[:, :, :, :], ALU.add).then_inc(stat_step, 1)
                    pool.wait_ge(stat_step, 5 * t + 2)
                    G.tensor_tensor(zr[:, 0, :, :], slots(unit), zer[:, 0, :, :], ALU.subtract).then_inc(stat_step, 1)
                    G.tensor_tensor(zr[:, 1, :, :], zer[:, 1, :, :], slots(unit), ALU.subtract).then_inc(stat_step, 1)
                    flat = scal[q][:, :, :, :].rearrange("p a s k -> p (a s k)")
                    rsqrt(flat, pw[:, :, :, :].rearrange("p a s k -> p (a s k)"), 24, stat_step)
                    pool.wait_ge(stat_step, 5 * t + 5)
                    G.tensor_tensor(scal[q][:, 1:3, :, :], scal[q][:, 1:3, :, :], zr[:, :, :, :], ALU.mult).then_inc(stat_sb, 1)
                if two_:
                    pool.wait_ge(mv2_sb, c(1))
                    l2_scale(0, 1, mv1[:, :, 0:1, 1], joint_step, 6 * u)
                    l3_scale(0, 1, mv1[:, :, 0:1, 1], joint_step, 6 * u, rC0_sb)
                if ending(t):
                    last_scale(t - 2, 1)

                def l0_scale(s):
                    pool.wait_ge(mv0_sb, a(s))
                    G.tensor_tensor(mv0[s][:, :, 1], mv0[s][:, :, 1], ln_eps[:, 0:NB], ALU.add).then_inc(l0_step, 1)
                    pool.wait_ge(l0_step, a(s))
                    rsqrt(rs0[s][:, :], mv0[s][:, :, 1], NB, rs0_sb)

                def l0_bias(s):
                    pool.wait_ge(x1_sb, a(s))
                    G.tensor_tensor(x1b[q][s][:, :, :], x1[s][:, :, :],
                                    bl1[:, :].rearrange("p (o d) -> p o d", o=1).to_broadcast([P, NB, D]),
                                    ALU.add).then_inc(x1b_sb, 1)

                if one:
                    l0_scale(0)
                    l0_scale(1)
                    l0_bias(0)
                    l0_bias(1)
                if ending(t):
                    last_scale(t - 1, 0)
                    last_scale(t - 1, 1)

            pairs_of(pool, body)


INPUTS = ['x', 'adj', 'L0_gnn_epsilon', 'L0_gnn_W1', 'L0_gnn_b1', 'L0_gnn_rms_weight', 'L0_gnn_W2', 'L0_gnn_b2',
          'L1_gnn_weight', 'L1_gnn_bias', 'L2_gnn_W1', 'L2_gnn_b1', 'L2_gnn_W2', 'L2_gnn_b2', 'L2_gnn_fusion_w',
          'L3_gnn_gamma', 'L3_gnn_beta', 'L3_gnn_W_self', 'L3_gnn_W_neigh']


def kernel(**inputs):
    import concourse.bacc as bacc
    from concourse.bass_utils import run_bass_kernel_spmd

    nc = bacc.Bacc("TRN2", target_bir_lowering=False, num_devices=1)
    arrays, args = {}, []
    for name in INPUTS:
        a = np.ascontiguousarray(np.asarray(inputs[name]))
        if a.ndim == 0 or name == 'L0_gnn_epsilon':
            a = a.reshape(1)
        arrays[name] = a
    arrays["shape_constants"] = shape_constants()
    for name, a in arrays.items():
        args.append(nc.dram_tensor(name, a.shape, mybir.dt.from_np(a.dtype), kind="ExternalInput").ap())
    out = nc.dram_tensor("out", (GRAPHS, NODES, D), mybir.dt.float32, kind="ExternalOutput").ap()
    build(nc, *args, out)
    r = run_bass_kernel_spmd(nc, [arrays], core_ids=[0])
    return r.results[0]["out"]
```
